# Optimizing a Trainium2 kernel written in Bass

```python
import numpy as np
import jax
import jax.numpy as jnp

def _softmax(x, axis=-1):
    return jax.nn.softmax(x, axis=axis)

def _gelu(x):
    return jax.nn.gelu(x, approximate=True)

def _silu(x):
    return jax.nn.silu(x)

def _sigmoid(x):
    return jax.nn.sigmoid(x)

def _layernorm(x, axis=-1, eps=1e-05):
    m = jnp.mean(x, axis=axis, keepdims=True)
    v = jnp.var(x, axis=axis, keepdims=True)
    return (x - m) / jnp.sqrt(v + eps)

def _scatter_add(tgt, idx, src, axis=0):
    return tgt.at[idx].add(src)

def _segment_sum(src, seg, n):
    return jax.ops.segment_sum(src, seg, n)
kernel_name = 'mk_gnn_resnorm_d1_gnn_r32_49bde0'

def setup_inputs(seed: int=0):
    np.random.seed(seed)
    _w = jnp.asarray

    def _rec_inputs():
        import jax
        import jax.numpy as jnp
        _gk = jax.random.key(seed)
        x = -0.0002117 + 1 * jax.random.normal(jax.random.fold_in(_gk, 1), (3125, 256), jnp.float32)
        _s = jax.random.randint(jax.random.fold_in(_gk, 2), (25000,), 0, 3125, jnp.int32)
        _d = jax.random.randint(jax.random.fold_in(_gk, 3), (25000,), 0, 3125, jnp.int32)
        _loop = jnp.arange(3125, dtype=jnp.int32)
        src = jnp.concatenate([_s, _d, _loop])
        dst = jnp.concatenate([_d, _s, _loop])
        _o = jnp.argsort(dst, stable=True)
        src = src[_o]
        dst = dst[_o]
        return (x, src, dst)
    x, src, dst = _rec_inputs()

    def _L0_gnn_setup():
        import jax, jax.numpy as jnp
        import numpy as np
        N_NODES = 3125

        def sage_conv(x, edge_index, Wl, bl, Wr):
            src, dst = (edge_index[0], edge_index[1])
            msg = x[src]
            agg = jax.ops.segment_sum(msg, dst, num_segments=N_NODES)
            cnt = jax.ops.segment_sum(jnp.ones((edge_index.shape[1],), x.dtype), dst, num_segments=N_NODES)
            agg = agg / jnp.maximum(cnt, 1.0)[:, None]
            return agg @ Wl.T + bl + x @ Wr.T
        key = jax.random.key(seed)
        ks = jax.random.split(key, 8)
        d_in, d_hid, d_out, E = (256, 512, 256, 10000)
        s = lambda k, shape, fan: jax.random.normal(k, shape, jnp.float32) * (1.0 / np.sqrt(fan))
        return {'x': jax.random.normal(ks[0], (N_NODES, d_in), jnp.float32), 'edge_index': jax.random.randint(ks[1], (2, E), 0, N_NODES, dtype=jnp.int64), 'W1l': s(ks[2], (d_hid, d_in), d_in), 'b1l': jnp.zeros((d_hid,), jnp.float32), 'W1r': s(ks[3], (d_hid, d_in), d_in), 'W2l': s(ks[4], (d_out, d_hid), d_hid), 'b2l': jnp.zeros((d_out,), jnp.float32), 'W2r': s(ks[5], (d_out, d_hid), d_hid)}
    _L0_gnn_all = _L0_gnn_setup()
    _L0_gnn_in = {k: v for k, v in _L0_gnn_all.items() if k in ('W1l', 'b1l', 'W1r', 'W2l', 'b2l', 'W2r')}
    del _L0_gnn_all
    return {'x': x, 'src': src, 'dst': dst, 'L0_gnn_W1l': _L0_gnn_in['W1l'], 'L0_gnn_b1l': _L0_gnn_in['b1l'], 'L0_gnn_W1r': _L0_gnn_in['W1r'], 'L0_gnn_W2l': _L0_gnn_in['W2l'], 'L0_gnn_b2l': _L0_gnn_in['b2l'], 'L0_gnn_W2r': _L0_gnn_in['W2r']}

def reference(x, src, dst, L0_gnn_W1l, L0_gnn_b1l, L0_gnn_W1r, L0_gnn_W2l, L0_gnn_b2l, L0_gnn_W2r):
    import jax
    import jax.numpy as jnp

    def _L0_gnn_ref(x, edge_index, W1l, b1l, W1r, W2l, b2l, W2r):
        import jax, jax.numpy as jnp
        import numpy as np
        N_NODES = 3125

        def sage_conv(x, edge_index, Wl, bl, Wr):
            src, dst = (edge_index[0], edge_index[1])
            msg = x[src]
            agg = jax.ops.segment_sum(msg, dst, num_segments=N_NODES)
            cnt = jax.ops.segment_sum(jnp.ones((edge_index.shape[1],), x.dtype), dst, num_segments=N_NODES)
            agg = agg / jnp.maximum(cnt, 1.0)[:, None]
            return agg @ Wl.T + bl + x @ Wr.T
        h = sage_conv(x, edge_index, W1l, b1l, W1r)
        h = jax.nn.relu(h)
        out = sage_conv(h, edge_index, W2l, b2l, W2r)
        return out
    edge_index = jnp.stack([src, dst])
    x = _layernorm(x + _L0_gnn_ref(x, edge_index, L0_gnn_W1l, L0_gnn_b1l, L0_gnn_W1r, L0_gnn_W2l, L0_gnn_b2l, L0_gnn_W2r), axis=-1)
    return x

_drawn_inputs = setup_inputs


def setup_inputs(seed=0):
    import zlib

    import numpy as np

    out = dict(_drawn_inputs(seed))
    spreads = {'L0_gnn_b1l': (0.0, 0.1), 'L0_gnn_b2l': (0.0, 0.1)}
    factors = {}
    for name, (base, spread) in spreads.items():
        noise = np.random.default_rng([zlib.crc32(name.encode()), seed]).standard_normal(out[name].shape)
        drawn = base * np.exp(spread * noise) if base else spread * noise
        out[name] = jnp.asarray(drawn.astype(out[name].dtype))
    for name, factor in factors.items():
        out[name] = (out[name] * factor).astype(out[name].dtype)
    return out
```

```python
import concourse.bass as bass
from concourse import mybir
from contextlib import ExitStack



def bass_sage_resnorm(nc: bass.Bass, x: bass.AP, src: bass.AP, dst: bass.AP, w1l: bass.AP, b1l: bass.AP,
                      w1r: bass.AP, w2l: bass.AP, b2l: bass.AP, w2r: bass.AP, out: bass.AP):
    fp32, fp16 = mybir.dt.float32, mybir.dt.float16
    i32, u32 = mybir.dt.int32, mybir.dt.uint32
    ALU = mybir.AluOpType
    ACT = mybir.ActivationFunctionType
    AX = mybir.AxisListType

    P = 128
    N, D = x.shape
    H = w1l.shape[0]
    E = src.shape[0]
    FT, HT = D // P, H // P
    ST = -(-N // P)
    NLAST = N - (ST - 1) * P
    WIN = 16
    NWIN = -(-N // WIN)
    KEYS = ST * WIN
    STEP = 512
    ROW = 32
    RPC = P // ROW
    CH = 3
    CAP = CH * RPC
    TR = -(-E // (P * ROW))
    EC = TR * ROW
    NROWS = P * TR
    EFULL = E // EC
    ETAIL = E - EFULL * EC
    FAR = 1 << 15
    SB = 512
    WPS, TPS = SB // WIN, SB // P
    NFULL = N // SB
    WLAST = NWIN - NFULL * WPS
    LASTW = WLAST * WIN
    GS = WPS * CH
    NG = NFULL + 1
    XC = 5
    EPS = 1e-5
    EXP_SUM = float((127 + 14 + 127) << 23)
    EXP_MASK = 0x7F800000
    TINY = 2.0 ** -100
    assert KEYS <= STEP and NLAST <= LASTW <= P and ST == NFULL * TPS + 1 and WPS % 2 == 0 and WLAST % 2 == 0
    assert GS <= P and ST % XC == 0

    rows_dram = nc.dram_tensor("edge_rows", [NROWS + P, 2 * ROW], fp32, kind="Internal").ap()
    wT_dram = nc.dram_tensor("weights_transposed", [P, 2 * FT * H + HT * 2 * D], fp32, kind="Internal").ap()
    strip0_dram = nc.dram_tensor("counts_strip0", [P, ST * SB], fp16, kind="Internal").ap()
    zr_dram = nc.dram_tensor("z_and_residual", [ST * P, 2 * D], fp32, kind="Internal").ap()

    ctx = ExitStack()
    with ctx:
        def sb(name, shape, dt):
            return ctx.enter_context(nc.sbuf_tensor(name, shape, dt))[:]

        def sem(name):
            return ctx.enter_context(nc.semaphore(name))

        def carve(words):
            at = [0]

            def take(n, dt=fp32):
                a, at[0] = at[0], at[0] + n
                assert at[0] <= words.shape[1], (at[0], words.shape)
                return words[:, a:at[0]] if dt is fp32 else words[:, a:at[0]].bitcast(dt)
            return take

        counts = sb("counts", [P, NFULL * ST * SB + ST * LASTW], fp16)
        parts = sb("parts", [P, ST, 2 * D], fp16)
        weights = sb("weights", [P, 2 * FT * H + HT * 2 * D], fp32)
        side = sb("side", [P, 1400], fp32)
        ident = sb("ident", [P, P], fp32)
        ones = sb("ones", [P, P], fp32)
        ones16 = sb("ones16", [P, P], fp16)
        b1T = sb("b1T", [P, HT], fp32)
        degree = sb("degree", [P, ST], fp32)
        rdegree = sb("rdegree", [P, ST], fp32)
        zmax = sb("zmax", [P, ST], fp32)
        amax = sb("amax", [P, 2], fp32)
        scale = sb("scale", [P, 4], fp32)
        srow = sb("srow", [1, 8], fp32)
        odd = sb("odd", [P, 1], fp32)
        frow = sb("frow", [1, 4], fp32)
        flag = sb("flag", [1, 1], i32)
        eps = sb("eps", [P, 1], fp32)
        stats = sb("stats", [P, TPS, 6], fp32)
        moments = sb("moments", [P, TPS, 2], fp32)
        deviation = sb("deviation", [P, TPS, 3], fp32)

        take = carve(weights)
        iota_key = take(KEYS // 2, fp16)
        iota_src = take(P // 2, fp16)
        hot_key = take(2 * CH * KEYS // 2, fp16).rearrange("p (r c) -> p r c", c=KEYS)
        hot_src = take(2 * CH * P // 2, fp16).rearrange("p (r c) -> p r c", c=P)
        zero16 = take(P // 2, fp16)
        w1T = weights[:, 0:2 * FT * H].rearrange("p (k h) -> p k h", h=H)
        w2T = weights[:, 2 * FT * H:].rearrange("p (m o) -> p m o", o=2 * D)
        take = carve(weights)
        z_in = [take(XC * D).rearrange("p (t f) -> p t f", f=D) for _ in range(2)]
        y = take(TPS * D).rearrange("p (n f) -> p n f", f=D)

        take = carve(side)
        rows = [take(2 * P).rearrange("p (i k e) -> p i k e", k=2, e=ROW) for _ in range(2)]
        unmixed = take(2 * P).rearrange("p (k e) -> p k e", k=2)
        slot_key = [take(GS) for _ in range(2)]
        slot_src = [take(GS) for _ in range(2)]
        key_base = take(GS)
        row_index = take(NG * RPC, u32)
        take = carve(side)
        all_keys, all_srcs = take(EC), take(EC)
        take = carve(side)
        xs = take(TPS * D).rearrange("p (n f) -> p n f", f=D)

        take = carve(counts[:, NFULL * ST * SB // 2:].bitcast(fp32))
        x_in = take(ST * D).rearrange("p (t f) -> p t f", f=D)
        w1_in = take(2 * HT * D).rearrange("p (k m f) -> p k m f", k=2, f=D)
        w2_in = take(2 * FT * H).rearrange("p (k o h) -> p k o h", k=2, h=H)
        keys = take(2 * EC).rearrange("p (r k e) -> p r k e", k=2, e=ROW)
        pad_rows = take(2 * ROW)
        dst_i, dst_next, src_i = take(EC, i32), take(EC, i32), take(EC, i32)
        k_win, k_dst, k_tile, k_src, k_sum = (take(EC, i32) for _ in range(5))
        disorder = take(EC)
        first_dst = take(TR)
        window_start = take(NWIN + 1)
        starts_below = take(TR * ((NWIN + 2) // 2), fp16).rearrange("p (t w) -> p t w", t=TR)[:, :, 0:NWIN + 1]
        rows_below = take(NWIN + 1)
        first_row = take(NWIN)
        row_span = take(NWIN)
        slot_row = take(NG * GS)
        slot_in = take(NG * GS)
        quarter = take(NG * RPC)

        take = carve(counts[:, 0:ST * SB].bitcast(fp32))
        hT = take(HT * SB).rearrange("p (m c) -> p m c", c=SB)
        aggT = take(FT * SB).rearrange("p (k c) -> p k c", c=SB)
        xT = take(FT * SB).rearrange("p (k c) -> p k c", c=SB)
        inv_degree = take(SB)
        max_degree = take(SB)
        z_out = take(2 * D).rearrange("p (b f) -> p b f", b=2)
        b2_row = take(D)

        bank = [ctx.enter_context(nc.psum_tensor(f"bank{i}", [P, 512], fp32))[:] for i in range(8)]

        def strip(s):
            return counts[:, bass.ds(s * (ST * SB), ST * SB)].rearrange("p (t c) -> p t c", c=SB)

        last_strip = counts[:, NFULL * ST * SB:].rearrange("p (t c) -> p t c", c=LASTW)

        def windows(bank_):
            return bank_[:, 0:KEYS].rearrange("p (t c) -> p t c", c=WIN)

        edges_in = sem("edges_in")
        x_loaded = sem("x_loaded")
        w_in = sem("w_in")
        bias_in = sem("bias_in")
        padded = sem("padded")
        consts = sem("consts")
        idents = sem("idents")
        prep = sem("prep")
        below_ready = sem("below_ready")
        rows_counted = sem("rows_counted")
        order_ready = sem("order_ready")
        order_summed = sem("order_summed")
        flag_ready = sem("flag_ready")
        keys_ready = sem("keys_ready")
        rows_stored = sem("rows_stored")
        slot_row_ready = sem("slot_row_ready")
        slot_row_turned = sem("slot_row_turned")
        index_ready = sem("index_ready")
        xmax_ready = sem("xmax_ready")
        max_turned = sem("max_turned")
        scale_row = sem("scale_row")
        scale_spread = sem("scale_spread")
        scale_ready = sem("scale_ready")
        high_ready = sem("high_ready")
        low_ready = sem("low_ready")
        w_turned = sem("w_turned")
        w_copied = sem("w_copied")
        w_stored = sem("w_stored")
        w_back = sem("w_back")
        gathered = [sem(f"gathered{b}") for b in range(2)]
        rows_unmixed = sem("rows_unmixed")
        rows_turned = sem("rows_turned")
        slots_ready = sem("slots_ready")
        hot_ready = sem("hot_ready")
        window_summed = sem("window_summed")
        window_stored = sem("window_stored")
        strip0_out = sem("strip0_out")
        strip0_back = sem("strip0_back")
        all_in = sem("all_in")
        all_keyed = sem("all_keyed")
        all_hot = sem("all_hot")
        all_used = sem("all_used")
        all_summed = sem("all_summed")
        all_stored = sem("all_stored")
        xs_in = sem("xs_in")
        turned = sem("turned")
        turned_copied = sem("turned_copied")
        agg_summed = sem("agg_summed")
        degree_ready = sem("degree_ready")
        inverse_ready = sem("inverse_ready")
        agg_ready = sem("agg_ready")
        h_summed = sem("h_summed")
        h_ready = sem("h_ready")
        zr_summed = sem("zr_summed")
        z_copied = sem("z_copied")
        r_added = sem("r_added")
        b2_in = sem("b2_in")
        b2_added = sem("b2_added")
        z_stored = [sem(f"z_stored{b}") for b in range(2)]
        r_stored = sem("r_stored")
        z_loaded = [sem(f"z_loaded{b}") for b in range(2)]
        zmax_ready = sem("zmax_ready")
        rdegree_ready = sem("rdegree_ready")
        out_summed = sem("out_summed")
        res_in = [sem(f"res_in{n}") for n in range(TPS)]
        high_joined = sem("high_joined")
        stats_ready = sem("stats_ready")
        root_inverted = sem("root_inverted")
        bank_read = sem("bank_read")
        moments_ready = sem("moments_ready")
        root_ready = sem("root_ready")
        factors_ready = sem("factors_ready")
        normed = sem("normed")
        out_stored = [sem(f"out_stored{n}") for n in range(TPS)]

        NSPLIT = ST // XC
        MAIN = E - ETAIL
        block = ctx.enter_context(nc.Block())

        def full_rows(ap, first=0):
            return ap[first:first + MAIN].rearrange("(p e) -> p e", e=EC)

        def tail_row(ap, first, n):
            return ap[first:first + n].rearrange("(p e) -> p e", p=1)

        def tile_of(q):
            if q < (NFULL - 1) * TPS:
                return 1 + q // TPS, q % TPS, P
            if q == (NFULL - 1) * TPS:
                return NFULL, 0, NLAST
            return 0, q - (NFULL - 1) * TPS - 1, P

        @block.sync
        def _(sp):
            sp.wait_ge(padded, 1)
            sp.dma_start(dst_i[0:EFULL, :], full_rows(dst)).then_inc(edges_in, 16)
            sp.dma_start(dst_i[EFULL:EFULL + 1, 0:ETAIL], tail_row(dst, MAIN, ETAIL)).then_inc(edges_in, 16)
            sp.dma_start(src_i[0:EFULL, :], full_rows(src)).then_inc(edges_in, 16)
            sp.dma_start(src_i[EFULL:EFULL + 1, 0:ETAIL], tail_row(src, MAIN, ETAIL)).then_inc(edges_in, 16)
            sp.dma_start(dst_next[0:EFULL, :], full_rows(dst, 1)).then_inc(edges_in, 16)
            sp.dma_start(dst_next[EFULL:EFULL + 1, 0:ETAIL - 1],
                         tail_row(dst, MAIN + 1, ETAIL - 1)).then_inc(edges_in, 16)
            sp.wait_ge(padded, 2)
            sp.dma_start(x_in[:, 0:ST - 1, :],
                         x[0:(ST - 1) * P, :].rearrange("(t p) f -> p t f", p=P)).then_inc(x_loaded, 16)
            sp.dma_start(x_in[0:NLAST, ST - 1, :], x[(ST - 1) * P:N, :]).then_inc(x_loaded, 16)
            sp.wait_ge(keys_ready, 2)
            sp.dma_start(rows_dram[0:NROWS, :].rearrange("(p r) c -> p (r c)", r=TR),
                         keys.rearrange("p r k e -> p (r k e)")).then_inc(rows_stored, 16)
            sp.dma_start(rows_dram[NROWS:NROWS + P, :], pad_rows).then_inc(rows_stored, 16)
            sp.wait_ge(w_copied, 2 * FT + 2 * HT // 2)
            sp.dma_start(wT_dram, weights).then_inc(w_stored, 16)

            sp.wait_ge(flag_ready, 1)
            slow = sp.value_load(flag[0:1, 0:1])
            with sp.If(slow > 0):
                sp.wait_ge(window_stored, NWIN)
                back = rows_dram[0:NROWS, :].rearrange("(p r) (k e) -> p r k e", r=TR, k=2)
                sp.dma_start(all_keys.rearrange("p (r e) -> p r e", e=ROW), back[:, :, 0, :]).then_inc(all_in, 16)
                sp.dma_start(all_srcs.rearrange("p (r e) -> p r e", e=ROW), back[:, :, 1, :]).then_inc(all_in, 16)
                sp.wait_ge(all_stored, NWIN)
            with sp.Else():
                sp.wait_ge(window_stored, NWIN)
            sp.dma_start(weights, wT_dram).then_inc(w_back, 16)
            sp.dma_start(strip0_dram, counts[:, 0:ST * SB]).then_inc(strip0_out, 16)

            def load_x(s):
                sp.dma_start(xs, x[bass.ds(s * SB, SB), :].rearrange("(n p) f -> p n f", p=P)).then_inc(xs_in, 16)

            def store_strip(s):
                for n in range(TPS):
                    sp.wait_ge(z_copied, s * TPS + n + 1)
                    sp.dma_start(zr_dram[bass.ds(s * SB + n * P, P), 0:D], z_out[:, n % 2, :])\
                        .then_inc(z_stored[n % 2], 16)
                sp.wait_ge(r_added, s * TPS + TPS)
                sp.dma_start(zr_dram[bass.ds(s * SB, SB), D:2 * D].rearrange("(n p) f -> p n f", p=P),
                             xs).then_inc(r_stored, 16)

            load_x(0)
            sp.wait_ge(strip0_out, 16)
            sp.wait_ge(agg_summed, 1)
            sp.dma_start(b2_row, b2l.partition_broadcast(P)).then_inc(b2_in, 16)
            store_strip(0)
            with sp.Fori(1, NFULL) as s:
                sp.wait_ge(r_stored, s * 16)
                load_x(s)
                store_strip(s)
            sp.wait_ge(r_stored, NFULL * 16)
            sp.dma_start(xs[0:NLAST, 0, :], x[NFULL * SB:N, :]).then_inc(xs_in, 16)
            sp.wait_ge(z_copied, NFULL * TPS + 1)
            sp.dma_start(zr_dram[NFULL * SB:N, 0:D], z_out[0:NLAST, 0, :]).then_inc(z_stored[0], 16)
            sp.wait_ge(r_added, NFULL * TPS + 1)
            sp.dma_start(zr_dram[NFULL * SB:N, D:2 * D], xs[0:NLAST, 0, :]).then_inc(r_stored, 16)

            sp.wait_ge(z_stored[0], 16 * (NFULL * TPS // 2 + 1))
            sp.wait_ge(z_stored[1], 16 * (NFULL * TPS // 2))
            sp.wait_ge(r_stored, 16 * NG)
            sp.wait_ge(zr_summed, NFULL * TPS + 1)
            for c in range(NSPLIT):
                if c >= 2:
                    sp.wait_ge(low_ready, NSPLIT + c - 1)
                full = XC if c < NSPLIT - 1 else XC - 1
                sp.dma_start(z_in[c % 2][:, 0:full, :],
                             zr_dram[c * XC * P:(c * XC + full) * P, 0:D].rearrange("(t p) f -> p t f", p=P))\
                    .then_inc(z_loaded[c % 2], 16)
                if full < XC:
                    sp.dma_start(z_in[c % 2][0:NLAST, full, :], zr_dram[(ST - 1) * P:N, 0:D])\
                        .then_inc(z_loaded[c % 2], 16)
            sp.dma_start(counts[:, 0:ST * SB], strip0_dram).then_inc(strip0_back, 16)

            def load_res(t, n, nodes):
                sp.dma_start(y[0:nodes, n, :], zr_dram[bass.ds(t * P, nodes), D:2 * D]).then_inc(res_in[n], 16)

            def store_out(q, t, n, nodes):
                sp.wait_ge(normed, q + 1)
                sp.dma_start(out[bass.ds(t * P, nodes), :], y[0:nodes, n, :]).then_inc(out_stored[n], 16)

            for n in range(TPS):
                load_res(TPS + n, n, P)
            with sp.Fori(1, NFULL - 1) as s:
                for n in range(TPS):
                    store_out((s - 1) * TPS + n, s * TPS + n, n, P)
                    sp.wait_ge(out_stored[n], s * 16)
                    load_res((s + 1) * TPS + n, n, P)
            for q in range((NFULL - 2) * TPS, ST):
                s, n, nodes = tile_of(q)
                store_out(q, s * TPS + n, q % TPS, nodes)
                if q + TPS < ST:
                    s, n, nodes = tile_of(q + TPS)
                    sp.wait_ge(out_stored[q % TPS], 16 * (q // TPS + 1))
                    load_res(s * TPS + n, q % TPS, nodes)
            for n in range(TPS):
                sp.wait_ge(out_stored[n], 16 * len(range(n, ST, TPS)))

        @block.gpsimd
        def _(pool):
            nc.gpsimd.memset(dst_i, FAR)
            nc.gpsimd.memset(dst_next, FAR)
            nc.gpsimd.memset(src_i, 0).then_inc(padded, 1)
            nc.gpsimd.memset(x_in[:, ST - 1, :], 0.0).then_inc(padded, 1)
            nc.gpsimd.memset(ident, 0.0).then_inc(idents, 1)
            nc.gpsimd.memset(ones, 1.0).then_inc(consts, 1)
            nc.gpsimd.memset(ones16, 1.0).then_inc(consts, 1)
            pool.wait_ge(idents, 1)
            nc.gpsimd.affine_select(out=ident, in_=ident, compare_op=ALU.not_equal, fill=1.0, base=0,
                                    pattern=[[-1, P]], channel_multiplier=1).then_inc(consts, 1)
            nc.gpsimd.iota(window_start, [[WIN, NWIN + 1]], base=0, channel_multiplier=0,
                           allow_small_or_imprecise_dtypes=True).then_inc(consts, 1)
            nc.gpsimd.iota(slot_in, [[0, NG * WPS], [RPC, CH]], base=0, channel_multiplier=0,
                           allow_small_or_imprecise_dtypes=True).then_inc(consts, 1)
            nc.gpsimd.iota(quarter, [[0, NG], [1, RPC]], base=0, channel_multiplier=0,
                           allow_small_or_imprecise_dtypes=True).then_inc(consts, 1)
            nc.gpsimd.iota(key_base, [[STEP, WPS], [0, CH]], base=0, channel_multiplier=0,
                           allow_small_or_imprecise_dtypes=True).then_inc(consts, 1)
            pool.wait_ge(w_stored, 16)
            nc.gpsimd.iota(iota_key, [[1, KEYS]], base=0, channel_multiplier=0,
                           allow_small_or_imprecise_dtypes=True).then_inc(consts, 1)
            nc.gpsimd.iota(iota_src, [[1, P]], base=0, channel_multiplier=0,
                           allow_small_or_imprecise_dtypes=True).then_inc(consts, 1)
            nc.gpsimd.memset(zero16, 0.0).then_inc(consts, 1)
            pool.wait_ge(rows_stored, 32)
            pool.wait_ge(index_ready, 1)
            for g in range(NG):
                if g >= 2:
                    pool.wait_ge(rows_unmixed, g - 1)
                for i in range(RPC):
                    nc.gpsimd.indirect_dma_start(
                        rows[g % 2][0:GS, i].rearrange("p k e -> p (k e)"), None, rows_dram,
                        bass.IndirectOffsetOnAxis(row_index[0:GS, g * RPC + i:g * RPC + i + 1], 0))\
                        .then_inc(gathered[g % 2], 16)

            def add_b2(s, nodes, n):
                b2 = b2_row[0:nodes, :].rearrange("p (o f) -> p o f", o=1).broadcast_to([nodes, n, D])
                nc.gpsimd.tensor_tensor(xs[0:nodes, 0:n, :], xs[0:nodes, 0:n, :], b2, ALU.add).then_inc(b2_added, 1)

            pool.wait_ge(b2_in, 16)
            pool.wait_ge(turned, FT)
            add_b2(0, P, TPS)
            with pool.Fori(1, NFULL) as s:
                pool.wait_ge(turned, s * (FT + 1) + FT)
                add_b2(s, P, TPS)
            pool.wait_ge(turned, NFULL * (FT + 1) + FT)
            add_b2(NFULL, NLAST, 1)

        @block.vector
        def _(dve):
            V = nc.vector
            steps = [0]

            def step(ins):
                ins.then_inc(prep, 1)
                steps[0] += 1
                dve.wait_ge(prep, steps[0])

            def find_scale(which, turns):
                dve.wait_ge(max_turned, turns)
                step(V.tensor_reduce(srow[0:1, 0:1], bank[3][0:1, 0:P], AX.X, ALU.max))
                step(V.tensor_scalar(srow[0:1, 1:2], srow[0:1, 0:1], TINY, None, ALU.max))
                step(V.tensor_scalar(srow[0:1, 2:3].bitcast(i32), srow[0:1, 1:2].bitcast(i32), EXP_MASK, None,
                                     ALU.bitwise_and))
                V.tensor_scalar(srow[0:1, 3:4].bitcast(i32), srow[0:1, 2:3].bitcast(i32), -1.0, EXP_SUM,
                                ALU.mult, ALU.add).then_inc(scale_row, 1)
                dve.wait_ge(scale_spread, turns)
                step(V.tensor_copy(scale[:, which:which + 1], bank[3][:, 256:257]))
                V.reciprocal(scale[:, 2 + which:3 + which], scale[:, which:which + 1]).then_inc(scale_ready, 1)

            V.memset(eps, EPS)
            V.memset(zmax, 0.0)
            V.memset(degree, 1.0)
            V.memset(pad_rows, -1.0).then_inc(keys_ready, 1)
            dve.wait_ge(edges_in, 6 * 16)
            V.tensor_scalar(k_win, dst_i, WIN.bit_length() - 1, STEP.bit_length() - 1,
                            ALU.arith_shift_right, ALU.logical_shift_left)
            V.tensor_scalar(k_dst, dst_i, WIN - 1, None, ALU.bitwise_and)
            V.tensor_scalar(k_tile, src_i, P.bit_length() - 1, WIN.bit_length() - 1,
                            ALU.arith_shift_right, ALU.logical_shift_left)
            V.tensor_scalar(k_src, src_i, P - 1, None, ALU.bitwise_and)
            step(V.tensor_copy(first_dst, dst_i[:, 0:EC:ROW]))
            step(V.tensor_tensor(k_sum, k_win, k_dst, ALU.add))
            V.tensor_tensor(keys[:, :, 0, :], k_sum.rearrange("p (r e) -> p r e", e=ROW),
                            k_tile.rearrange("p (r e) -> p r e", e=ROW), ALU.add)
            V.tensor_copy(keys[:, :, 1, :], k_src.rearrange("p (r e) -> p r e", e=ROW)).then_inc(keys_ready, 1)
            dve.wait_ge(consts, 4)
            for t in range(TR):
                ins = V.tensor_scalar(starts_below[:, t, :], window_start, first_dst[:, t:t + 1], None, ALU.is_gt)
            ins.then_inc(below_ready, 1)
            step(V.tensor_tensor(disorder, dst_i, dst_next, ALU.is_gt))
            V.tensor_reduce(odd, disorder, AX.X, ALU.add).then_inc(order_ready, 1)
            dve.wait_ge(rows_counted, 1)
            step(V.tensor_copy(rows_below[0:1, :], bank[2][0:1, 0:NWIN + 1]))
            step(V.tensor_scalar(first_row[0:1, :], rows_below[0:1, 0:NWIN], -1.0, 0.0, ALU.add, ALU.max))
            V.memset(slot_row[0:1, NWIN * CH:], 0.0)
            dve.wait_ge(consts, 6)
            first3 = first_row[0:1, :].rearrange("p (w o) -> p w o", o=1).broadcast_to([1, NWIN, CH])
            V.tensor_tensor(slot_row[0:1, 0:NWIN * CH].rearrange("p (w c) -> p w c", c=CH), first3,
                            slot_in[0:1, 0:NWIN * CH].rearrange("p (w c) -> p w c", c=CH), ALU.add)\
                .then_inc(slot_row_ready, 1)
            step(V.tensor_tensor(row_span[0:1, :], rows_below[0:1, 1:], first_row[0:1, :], ALU.subtract))
            step(V.tensor_reduce(frow[0:1, 0:1], row_span[0:1, :], AX.X, ALU.max))
            step(V.tensor_scalar(frow[0:1, 1:2], frow[0:1, 0:1], float(CAP), None, ALU.is_gt))
            dve.wait_ge(order_summed, 1)
            dve.wait_ge(slot_row_turned, 1)
            V.tensor_tensor(flag, frow[0:1, 1:2], bank[2][0:1, 256:257], ALU.add).then_inc(flag_ready, 1)
            V.tensor_tensor(row_index[0:GS, :], bank[2][0:GS, 320:320 + NG * RPC], quarter[0:GS, :],
                            ALU.add).then_inc(index_ready, 1)

            dve.wait_ge(x_loaded, 32)
            V.tensor_reduce(amax[:, 0:1], x_in.rearrange("p t f -> p (t f)"), AX.X, ALU.max,
                            apply_absolute_value=True).then_inc(xmax_ready, 1)
            find_scale(0, 1)

            def low_part(c, value, nodes, t0, n, which):
                rest = parts[0:nodes, t0:t0 + n, D:2 * D]
                return V.scalar_tensor_tensor(out=rest, in0=value, scalar=scale[0:nodes, which:which + 1],
                                              in1=parts[0:nodes, t0:t0 + n, 0:D], op0=ALU.mult, op1=ALU.subtract)

            for c in range(NSPLIT):
                dve.wait_ge(high_ready, c + 1)
                low_part(c, x_in[:, c * XC:(c + 1) * XC, :], P, c * XC, XC, 0).then_inc(low_ready, 1)

            dve.wait_ge(consts, 10)

            def window_hots(g, w, buf):
                for j in range(CH):
                    r = buf * CH + j
                    V.tensor_scalar(hot_key[:, r, :], iota_key, slot_key[g % 2][:, bass.ds(w * CH + j, 1)],
                                    None, ALU.is_equal)
                    V.tensor_scalar(hot_src[:, r, :], iota_src, slot_src[g % 2][:, bass.ds(w * CH + j, 1)],
                                    None, ALU.is_equal).then_inc(hot_ready, 1)

            for g in range(NG):
                nwin = WPS if g < NFULL else WLAST
                dve.wait_ge(rows_turned, g + 1)
                V.scalar_tensor_tensor(out=slot_key[g % 2], in0=bank[4 + g % 2][:, 0:GS],
                                       scalar=float(-STEP * WPS * g), in1=key_base, op0=ALU.add, op1=ALU.subtract)
                V.tensor_copy(slot_src[g % 2], bank[4 + g % 2][:, P:P + GS]).then_inc(slots_ready, 1)
                dve.wait_ge(slots_ready, g + 1)
                if g == 0:
                    window_hots(g, 0, 0)
                    window_hots(g, 1, 1)
                with dve.Fori(1 if g == 0 else 0, nwin // 2) as pair:
                    for b in range(2):
                        dve.wait_ge(window_summed, pair * 2 + (g * WPS + b - 1))
                        window_hots(g, pair * 2 + b, b)

            slow = dve.value_load(flag[0:1, 0:1])
            with dve.If(slow > 0):
                dve.wait_ge(all_in, 32)
                with dve.Fori(0, NWIN) as w:
                    with dve.Fori(0, EC // 4) as c:
                        dve.wait_ge(all_used, w * (EC // 4) + c + 1)
                        for j in range(4):
                            V.tensor_scalar(hot_key[:, j, :], iota_key, all_keys[:, bass.ds(c * 4 + j, 1)], None,
                                            ALU.is_equal)
                            ins = V.tensor_scalar(hot_src[:, j, :], iota_src, all_srcs[:, bass.ds(c * 4 + j, 1)],
                                                  None, ALU.is_equal)
                        ins.then_inc(all_hot, 1)
                    dve.wait_ge(all_hot, w * (EC // 4) + EC // 4)
                    V.tensor_scalar(all_keys, all_keys, float(-STEP), None, ALU.add).then_inc(all_keyed, 1)
                    dve.wait_ge(all_keyed, w + 1)
            with dve.Else():
                dve.wait_ge(flag_ready, 1)

            def aggregate(s, cols, first):
                dve.wait_ge(agg_summed, s + 1)
                if first:
                    dve.wait_ge(strip0_out, 16)
                else:
                    dve.wait_ge(turned, s * (FT + 1))
                    dve.wait_ge(h_summed, s * HT)
                V.tensor_scalar(max_degree[:, 0:cols], bank[2][:, 0:cols], 1.0, None, ALU.max)\
                    .then_inc(degree_ready, 1)
                dve.wait_ge(degree_ready, s + 1)
                V.reciprocal(inv_degree[:, 0:cols], max_degree[:, 0:cols]).then_inc(inverse_ready, 1)
                dve.wait_ge(inverse_ready, s + 1)
                for k in range(FT):
                    V.scalar_tensor_tensor(out=aggT[:, k, 0:cols], in0=bank[k][:, 0:cols], scalar=scale[:, 2:3],
                                           in1=inv_degree[:, 0:cols], op0=ALU.mult, op1=ALU.mult)\
                        .then_inc(agg_ready, 1)

            def residual(s, n, nodes):
                b = bank[5 + n % 2]
                dve.wait_ge(z_copied, s * TPS + n + 1)
                V.tensor_reduce(zmax[0:nodes, bass.ds(s * TPS + n, 1)], b[0:nodes, 0:D], AX.X, ALU.max,
                                apply_absolute_value=True)
                V.tensor_tensor(xs[0:nodes, n, :], b[0:nodes, D:2 * D], xs[0:nodes, n, :], ALU.add)\
                    .then_inc(r_added, 1)

            def residuals(s, tiles, nodes):
                dve.wait_ge(b2_added, s + 1)
                for n in range(tiles):
                    residual(s, n, nodes)

            aggregate(0, SB, True)
            aggregate(1, SB, False)
            residuals(0, TPS, P)
            with dve.Fori(1, NFULL - 1) as s:
                aggregate(s + 1, SB, False)
                residuals(s, TPS, P)
            aggregate(NFULL, NLAST, False)
            residuals(NFULL - 1, TPS, P)
            residuals(NFULL, 1, NLAST)

            dve.wait_ge(r_added, NFULL * TPS + 1)
            V.tensor_reduce(amax[:, 1:2], zmax, AX.X, ALU.max).then_inc(zmax_ready, 1)
            find_scale(1, 2)
            dve.wait_ge(turned_copied, NG * (FT + 1))
            step(V.reciprocal(rdegree, degree))
            dve.wait_ge(scale_ready, 2)
            V.tensor_scalar(rdegree, rdegree, scale[:, 3:4], None, ALU.mult).then_inc(rdegree_ready, 1)
            for c in range(NSPLIT):
                dve.wait_ge(high_ready, NSPLIT + c + 1)
                if c < NSPLIT - 1:
                    low_part(c, z_in[c % 2], P, c * XC, XC, 1).then_inc(low_ready, 1)
                else:
                    low_part(c, z_in[c % 2][:, 0:XC - 1, :], P, c * XC, XC - 1, 1)
                    low_part(c, z_in[c % 2][0:NLAST, XC - 1:XC, :], NLAST, ST - 1, 1, 1).then_inc(low_ready, 1)
            dve.wait_ge(rdegree_ready, 1)

            def join(q, t, n, nodes, loads):
                b, row = bank[n], y[0:nodes, n, :]
                dve.wait_ge(out_summed, q + 1)
                dve.wait_ge(res_in[n], loads)
                V.scalar_tensor_tensor(out=row, in0=b[0:nodes, 0:D], scalar=rdegree[0:nodes, bass.ds(t, 1)],
                                       in1=row, op0=ALU.mult, op1=ALU.add).then_inc(high_joined, 1)
                dve.wait_ge(high_joined, q + 1)
                V.scalar_tensor_tensor(out=row, in0=b[0:nodes, D:2 * D], scalar=rdegree[0:nodes, bass.ds(t, 1)],
                                       in1=row, op0=ALU.mult, op1=ALU.add).then_inc(bank_read, 1)
                dve.wait_ge(bank_read, q + 1)
                V.bn_stats(stats[0:nodes, n, :], row).then_inc(stats_ready, 1)

            def root(q, n, nodes):
                dve.wait_ge(root_ready, q + 1)
                V.reciprocal(deviation[0:nodes, n, 1:2], deviation[0:nodes, n, 0:1]).then_inc(root_inverted, 1)

            def aggregate_stats(n, nodes):
                V.bn_aggr(moments[0:nodes, n, :], stats[0:nodes, n, :]).then_inc(moments_ready, 1)

            def factor(q, n, nodes):
                dve.wait_ge(root_inverted, q + 1)
                V.scalar_tensor_tensor(out=deviation[0:nodes, n, 2:3], in0=moments[0:nodes, n, 0:1], scalar=-1.0,
                                       in1=deviation[0:nodes, n, 1:2], op0=ALU.mult, op1=ALU.mult)\
                    .then_inc(factors_ready, 1)

            def finish(q, t, n, nodes, loads):
                join(q, t, n, nodes, loads)
                dve.wait_ge(stats_ready, q + 1)
                root(q - 1, (n - 1) % TPS, P)
                aggregate_stats(n, nodes)
                factor(q - 1, (n - 1) % TPS, P)

            join(0, TPS, 0, P, 16)
            dve.wait_ge(stats_ready, 1)
            aggregate_stats(0, P)
            for n in range(1, TPS):
                finish(n, TPS + n, n, P, 16)
            with dve.Fori(1, NFULL - 1) as s:
                for n in range(TPS):
                    finish(s * TPS + n, (s + 1) * TPS + n, n, P, s * 16 + 16)
            for q in range((NFULL - 1) * TPS, ST):
                s, n, nodes = tile_of(q)
                join(q, s * TPS + n, q % TPS, nodes, 16 * (q // TPS + 1))
                dve.wait_ge(stats_ready, q + 1)
                before = tile_of(q - 1)[2]
                root(q - 1, (q - 1) % TPS, before)
                aggregate_stats(q % TPS, nodes)
                factor(q - 1, (q - 1) % TPS, before)
            root(ST - 1, (ST - 1) % TPS, P)
            factor(ST - 1, (ST - 1) % TPS, P)

        @block.scalar
        def _(act):
            A = nc.scalar
            act.dma_start(w1_in[:, 0], w1l.rearrange("(m p) f -> p m f", p=P)).then_inc(w_in, 16)
            act.dma_start(w1_in[:, 1], w1r.rearrange("(m p) f -> p m f", p=P)).then_inc(w_in, 16)
            act.dma_start(w2_in[:, 0], w2l.rearrange("(o p) h -> p o h", p=P)).then_inc(w_in, 16)
            act.dma_start(w2_in[:, 1], w2r.rearrange("(o p) h -> p o h", p=P)).then_inc(w_in, 16)
            act.dma_start(b1T, b1l.rearrange("(m p) -> p m", p=P), allow_slow_non_contiguous=True).then_inc(bias_in, 16)
            for k in range(8):
                act.wait_ge(w_turned, k + 1)
                to = w1T[:, k, :] if k < 2 * FT else w2T[:, k - 2 * FT, :]
                A.copy(to, bank[k % 2]).then_inc(w_copied, 1)

            def high_part(value, nodes, t0, n, which):
                return A.activation(parts[0:nodes, t0:t0 + n, 0:D], value, ACT.Copy,
                                    scale=scale[0:nodes, which:which + 1])

            act.wait_ge(scale_ready, 1)
            for c in range(NSPLIT):
                high_part(x_in[:, c * XC:(c + 1) * XC, :], P, c * XC, XC, 0).then_inc(high_ready, 1)

            def unmix(g):
                act.wait_ge(gathered[g % 2], 16 * RPC * (g // 2 + 1))
                if g >= 1:
                    act.wait_ge(rows_turned, g)
                A.copy(unmixed[0:GS].rearrange("p k (i e) -> p k i e", e=ROW),
                       rows[g % 2][0:GS].rearrange("p i k e -> p k i e")).then_inc(rows_unmixed, 1)

            def store_window(where, w, b, done, summed, stored):
                act.wait_ge(summed, done + 1)
                A.copy(where[:, :, bass.ds(w * WIN, WIN)], windows(bank[6 + b])).then_inc(stored, 1)

            unmix(0)
            unmix(1)
            act.wait_ge(low_ready, NSPLIT)
            for g in range(NG):
                if 1 <= g < NFULL:
                    unmix(g + 1)
                nwin = WPS if g < NFULL else WLAST
                where = strip(g) if g < NFULL else last_strip
                with act.Fori(0, nwin // 2) as pair:
                    for b in range(2):
                        store_window(where, pair * 2 + b, b, pair * 2 + (g * WPS + b), window_summed, window_stored)

            slow = act.value_load(flag[0:1, 0:1])
            with act.If(slow > 0):
                with act.Fori(0, NFULL) as s:
                    with act.Fori(0, WPS) as w:
                        store_window(strip(s), w, 0, s * WPS + w, all_summed, all_stored)
                with act.Fori(0, WLAST) as w:
                    store_window(last_strip, w, 0, w + NFULL * WPS, all_summed, all_stored)
            with act.Else():
                act.wait_ge(flag_ready, 1)

            def copy_xT(s, k, cols):
                act.wait_ge(turned, s * (FT + 1) + k + 1)
                A.copy(xT[:, k, 0:cols], bank[7][:, 0:cols]).then_inc(turned_copied, 1)

            def copy_degree(s, tiles, nodes):
                act.wait_ge(turned, s * (FT + 1) + FT + 1)
                A.copy(degree[0:nodes, bass.ds(s * TPS, tiles)], bank[7][0:nodes, 0:tiles]).then_inc(turned_copied, 1)

            def hidden(s, cols, first):
                if not first:
                    act.wait_ge(zr_summed, s * TPS)
                for m in range(HT):
                    act.wait_ge(h_summed, s * HT + m + 1)
                    A.activation(hT[:, m, 0:cols], bank[3 + m % 2][:, 0:cols], ACT.Relu, bias=b1T[:, m:m + 1])\
                        .then_inc(h_ready, 1)

            def copy_z(s, tiles, nodes, first):
                for n in range(tiles):
                    act.wait_ge(zr_summed, s * TPS + n + 1)
                    if not first:
                        act.wait_ge(z_stored[n % 2], s * (16 * TPS // 2) + 16 * (n // 2))
                    elif n >= 2:
                        act.wait_ge(z_stored[n % 2], 16 * (n // 2))
                    A.copy(z_out[0:nodes, n % 2, :], bank[5 + n % 2][0:nodes, 0:D]).then_inc(z_copied, 1)

            def strip_steps(s, tiles, nodes, cols, first=False):
                copy_degree(s, tiles, nodes)
                hidden(s, cols, first)
                copy_z(s, tiles, nodes, first)

            def copy_xTs(s, cols):
                for k in range(FT):
                    copy_xT(s, k, cols)

            act.wait_ge(bias_in, 16)
            act.wait_ge(strip0_out, 16)
            act.wait_ge(agg_summed, 1)
            copy_xTs(0, SB)
            strip_steps(0, TPS, P, SB, True)
            with act.Fori(1, NFULL) as s:
                copy_xTs(s, SB)
                strip_steps(s, TPS, P, SB)
            copy_xTs(NFULL, NLAST)
            strip_steps(NFULL, 1, NLAST, NLAST)

            act.wait_ge(scale_ready, 2)
            for c in range(NSPLIT):
                if c < NSPLIT - 1:
                    act.wait_ge(z_loaded[c % 2], 16 * (c // 2 + 1))
                    high_part(z_in[c % 2], P, c * XC, XC, 1).then_inc(high_ready, 1)
                else:
                    act.wait_ge(z_loaded[c % 2], 16 * (c // 2 + 2))
                    high_part(z_in[c % 2][:, 0:XC - 1, :], P, c * XC, XC - 1, 1)
                    high_part(z_in[c % 2][0:NLAST, XC - 1:XC, :], NLAST, ST - 1, 1, 1).then_inc(high_ready, 1)

            def norm(q, n, nodes):
                act.wait_ge(moments_ready, q + 1)
                A.activation(deviation[0:nodes, n, 0:1], moments[0:nodes, n, 1:2], ACT.Sqrt, bias=eps[0:nodes, :])\
                    .then_inc(root_ready, 1)
                act.wait_ge(factors_ready, q + 1)
                A.activation(y[0:nodes, n, :], y[0:nodes, n, :], ACT.Identity, scale=deviation[0:nodes, n, 1:2],
                             bias=deviation[0:nodes, n, 2:3]).then_inc(normed, 1)

            with act.Fori(0, NFULL - 1) as s:
                for n in range(TPS):
                    norm(s * TPS + n, n, P)
            for q in range((NFULL - 1) * TPS, ST):
                norm(q, q % TPS, tile_of(q)[2])

        @block.tensor
        def _(pe):
            T = nc.tensor

            def mm(o, a, b, start=True, stop=True):
                return T.matmul(o, a, b, start=start, stop=stop)

            pe.wait_ge(consts, 3)
            pe.wait_ge(w_in, 4 * 16)
            for k in range(8):
                if k >= 2:
                    pe.wait_ge(w_copied, k - 1)
                for i in range(4):
                    if k < 2 * FT:
                        tile = w1_in[:, k // FT, i, (k % FT) * P:(k % FT + 1) * P]
                    else:
                        tile = w2_in[:, i // FT, i % FT, (k - 2 * FT) * P:(k - 2 * FT + 1) * P]
                    ins = T.transpose(bank[k % 2][:, i * P:(i + 1) * P], tile, ident)
                ins.then_inc(w_turned, 1)
            pe.wait_ge(below_ready, 1)
            for t in range(TR):
                ins = mm(bank[2][0:1, 0:NWIN + 1], ones16[:, 0:1], starts_below[:, t, :], t == 0, t == TR - 1)
            ins.then_inc(rows_counted, 1)
            pe.wait_ge(order_ready, 1)
            pe.wait_ge(slot_row_ready, 1)
            mm(bank[2][0:1, 256:257], odd, ones[:, 0:1]).then_inc(order_summed, 1)
            for g in range(NG):
                ins = mm(bank[2][0:GS, 320 + g * RPC:320 + (g + 1) * RPC], slot_row[0:1, g * GS:(g + 1) * GS],
                         ones[0:1, 0:RPC])
            ins.then_inc(slot_row_turned, 1)

            def spread_scale(which):
                T.transpose(bank[3][0:1, 0:P], amax[:, which:which + 1], ident).then_inc(max_turned, 1)
                pe.wait_ge(scale_row, which + 1)
                mm(bank[3][:, 256:257], ones[0:1, :], srow[0:1, 3:4]).then_inc(scale_spread, 1)

            pe.wait_ge(xmax_ready, 1)
            spread_scale(0)

            def turn_rows(g):
                pe.wait_ge(rows_unmixed, g + 1)
                if g >= 2:
                    pe.wait_ge(slots_ready, g - 1)
                for k in range(2):
                    ins = T.transpose(bank[4 + g % 2][:, k * P:k * P + GS], unmixed[0:GS, k, :], ident[0:GS, 0:GS])
                ins.then_inc(rows_turned, 1)

            def sum_window(b, done, free):
                if free is not None:
                    pe.wait_ge(window_stored, free)
                for j in range(CH):
                    pe.wait_ge(hot_ready, done * CH + j + 1)
                    ins = mm(bank[6 + b][:, 0:KEYS], hot_src[:, b * CH + j, :], hot_key[:, b * CH + j, :],
                             j == 0, j == CH - 1)
                ins.then_inc(window_summed, 1)

            turn_rows(0)
            for g in range(NG):
                if g + 1 < NG:
                    turn_rows(g + 1)
                if g == 0:
                    sum_window(0, 0, None)
                    sum_window(1, 1, None)
                with pe.Fori(1 if g == 0 else 0, (WPS if g < NFULL else WLAST) // 2) as pair:
                    for b in range(2):
                        sum_window(b, pair * 2 + (g * WPS + b), pair * 2 + (g * WPS + b - 1))

            pe.wait_ge(flag_ready, 1)
            slow = pe.value_load(flag[0:1, 0:1])
            with pe.If(slow > 0):
                pe.wait_ge(window_stored, NWIN)
                mm(bank[6][:, 0:KEYS], zero16, iota_key).then_inc(all_used, 1)
                with pe.Fori(0, NWIN) as w:
                    mm(bank[6][:, 0:KEYS], zero16, iota_key, True, False)
                    with pe.Fori(0, EC // 4) as c:
                        pe.wait_ge(all_hot, w * (EC // 4) + c + 1)
                        for j in range(4):
                            ins = mm(bank[6][:, 0:KEYS], hot_src[:, j, :], hot_key[:, j, :], False, False)
                        ins.then_inc(all_used, 1)
                    mm(bank[6][:, 0:KEYS], zero16, iota_key, False, True).then_inc(all_summed, 1)
                    pe.wait_ge(all_stored, w + 1)
            with pe.Else():
                pe.wait_ge(window_stored, NWIN)

            def aggregate(s, where, cols, first=False):
                if not first:
                    pe.wait_ge(agg_ready, s * FT)
                for t in range(ST):
                    for k in range(FT):
                        for part in range(2):
                            a = part * D + k * P
                            mm(bank[k][:, 0:cols], parts[:, t, a:a + P], where[:, t, 0:cols],
                               t == 0 and part == 0, t == ST - 1 and part == 1)
                    ins = mm(bank[2][:, 0:cols], ones16, where[:, t, 0:cols], t == 0, t == ST - 1)
                ins.then_inc(agg_summed, 1)

            def turn_x(s, tiles, nodes, first=False):
                pe.wait_ge(xs_in, s * 16 + 16)
                for k in range(FT):
                    if k or not first:
                        pe.wait_ge(turned_copied, s * (FT + 1) + k)
                    for n in range(tiles):
                        ins = T.transpose(bank[7][:, n * P:n * P + nodes], xs[0:nodes, n, k * P:(k + 1) * P],
                                          ident[0:nodes, 0:nodes])
                    ins.then_inc(turned, 1)

            def turn_degree(s, tiles, nodes):
                pe.wait_ge(degree_ready, s + 1)
                pe.wait_ge(turned_copied, s * (FT + 1) + FT)
                for n in range(tiles):
                    ins = mm(bank[7][0:nodes, n:n + 1], max_degree[0:1, n * P:n * P + nodes], ones[0:1, 0:1])
                ins.then_inc(turned, 1)

            def hidden(s, cols, first=False):
                pe.wait_ge(agg_ready, s * FT + FT)
                for m in range(HT):
                    if m >= 2 or not first:
                        pe.wait_ge(h_ready, s * HT + (m - 1))
                    for k in range(2 * FT):
                        operand = aggT[:, k, 0:cols] if k < FT else xT[:, k - FT, 0:cols]
                        ins = mm(bank[3 + m % 2][:, 0:cols], w1T[:, k, m * P:(m + 1) * P], operand,
                                 k == 0, k == 2 * FT - 1)
                    ins.then_inc(h_summed, 1)

            def outputs(s, tiles, nodes, first=False):
                pe.wait_ge(h_ready, s * HT + HT)
                for n in range(tiles):
                    if n >= 2 or not first:
                        pe.wait_ge(z_copied, s * TPS + (n - 1))
                        pe.wait_ge(r_added, s * TPS + (n - 1))
                    for m in range(HT):
                        ins = mm(bank[5 + n % 2][0:nodes, :], hT[:, m, n * P:n * P + nodes], w2T[:, m, :],
                                 m == 0, m == HT - 1)
                    ins.then_inc(zr_summed, 1)

            pe.wait_ge(low_ready, NSPLIT)
            aggregate(0, strip(0), SB, True)
            turn_x(0, TPS, P, True)
            aggregate(1, strip(1), SB)
            turn_degree(0, TPS, P)
            pe.wait_ge(w_back, 16)
            hidden(0, SB, True)
            outputs(0, TPS, P, True)
            with pe.Fori(1, NFULL - 1) as s:
                turn_x(s, TPS, P)
                aggregate(s + 1, strip(s + 1), SB)
                turn_degree(s, TPS, P)
                hidden(s, SB)
                outputs(s, TPS, P)
            turn_x(NFULL - 1, TPS, P)
            aggregate(NFULL, last_strip, NLAST)
            turn_degree(NFULL - 1, TPS, P)
            hidden(NFULL - 1, SB)
            outputs(NFULL - 1, TPS, P)
            turn_x(NFULL, 1, NLAST)
            turn_degree(NFULL, 1, NLAST)
            hidden(NFULL, NLAST)
            outputs(NFULL, 1, NLAST)

            pe.wait_ge(zmax_ready, 1)
            spread_scale(1)

            def sum_out(q, where, col, n, nodes, first=False):
                if not first:
                    pe.wait_ge(bank_read, q - (TPS - 1))
                for t in range(ST):
                    ins = mm(bank[n][0:nodes, :], where[:, t, col:col + nodes], parts[:, t, :], t == 0, t == ST - 1)
                ins.then_inc(out_summed, 1)

            pe.wait_ge(low_ready, 2 * NSPLIT)
            pe.wait_ge(scale_ready, 2)
            for n in range(TPS):
                sum_out(n, strip(1), n * P, n, P, True)
            with pe.Fori(1, NFULL - 1) as s:
                for n in range(TPS):
                    sum_out(s * TPS + n, strip(s + 1), n * P, n, P)
            for q in range((NFULL - 1) * TPS, ST):
                s, n, nodes = tile_of(q)
                if s == 0 and n == 0:
                    pe.wait_ge(strip0_back, 16)
                sum_out(q, last_strip if s else strip(0), n * P, q % TPS, nodes)


_INS = ["x", "src", "dst", "L0_gnn_W1l", "L0_gnn_b1l", "L0_gnn_W1r", "L0_gnn_W2l", "L0_gnn_b2l", "L0_gnn_W2r"]


def kernel(**inputs):
    import numpy as _np
    import concourse.bacc as _bacc
    from concourse import mybir as _mybir
    from concourse.bass_utils import run_bass_kernel_spmd as _run

    nc = _bacc.Bacc("TRN2", target_bir_lowering=False, num_devices=1)
    arrays, args = {}, []
    for name in _INS:
        a = _np.ascontiguousarray(inputs[name])
        arrays[f"in_{name}"] = a
        args.append(nc.dram_tensor(f"in_{name}", a.shape, _mybir.dt.from_np(a.dtype), kind="ExternalInput").ap())
    shape = inputs["x"].shape
    args.append(nc.dram_tensor("out_dram", shape, _mybir.dt.float32, kind="ExternalOutput").ap())
    bass_sage_resnorm(nc, *args)
    r = _run(nc, [arrays], core_ids=[0])
    return r.results[0]["out_dram"]
```

```python
import concourse.bass as bass
from concourse import mybir
from contextlib import ExitStack



def bass_sage_resnorm(nc: bass.Bass, x: bass.AP, src: bass.AP, dst: bass.AP, w1l: bass.AP, b1l: bass.AP,
                      w1r: bass.AP, w2l: bass.AP, b2l: bass.AP, w2r: bass.AP, out: bass.AP):
    fp32, fp16 = mybir.dt.float32, mybir.dt.float16
    i32, u32 = mybir.dt.int32, mybir.dt.uint32
    ALU = mybir.AluOpType
    ACT = mybir.ActivationFunctionType
    AX = mybir.AxisListType

    P = 128
    N, D = x.shape
    H = w1l.shape[0]
    E = src.shape[0]
    FT, HT = D // P, H // P
    ST = -(-N // P)
    NLAST = N - (ST - 1) * P
    WIN = 16
    NWIN = -(-N // WIN)
    KEYS = ST * WIN
    STEP = 512
    ROW = 32
    RPC = P // ROW
    CH = 3
    CAP = CH * RPC
    TR = -(-E // (P * ROW))
    EC = TR * ROW
    NROWS = P * TR
    EFULL = E // EC
    ETAIL = E - EFULL * EC
    FAR = 1 << 15
    SB = 512
    WPS, TPS = SB // WIN, SB // P
    NFULL = N // SB
    WLAST = NWIN - NFULL * WPS
    LASTW = WLAST * WIN
    GS = WPS * CH
    NG = NFULL + 1
    XC = 5
    EPS = 1e-5
    EXP_SUM = float((127 + 14 + 127) << 23)
    EXP_MASK = 0x7F800000
    TINY = 2.0 ** -100
    assert KEYS <= STEP and NLAST <= LASTW <= P and ST == NFULL * TPS + 1 and WPS % 2 == 0 and WLAST % 2 == 0
    assert GS <= P and ST % XC == 0

    rows_dram = nc.dram_tensor("edge_rows", [NROWS + P, 2 * ROW], fp32, kind="Internal").ap()
    wT_dram = nc.dram_tensor("weights_transposed", [P, 2 * FT * H + HT * 2 * D], fp32, kind="Internal").ap()
    early_dram = nc.dram_tensor("counts_strips01", [2, P, ST * SB], fp16, kind="Internal").ap()
    zr_dram = nc.dram_tensor("z_and_residual", [ST * P, 2 * D], fp32, kind="Internal").ap()

    ctx = ExitStack()
    with ctx:
        def sb(name, shape, dt):
            return ctx.enter_context(nc.sbuf_tensor(name, shape, dt))[:]

        def sem(name):
            return ctx.enter_context(nc.semaphore(name))

        def carve(words):
            at = [0]

            def take(n, dt=fp32):
                a, at[0] = at[0], at[0] + n
                assert at[0] <= words.shape[1], (at[0], words.shape)
                return words[:, a:at[0]] if dt is fp32 else words[:, a:at[0]].bitcast(dt)
            return take

        counts = sb("counts", [P, NFULL * ST * SB + ST * LASTW], fp16)
        parts = sb("parts", [P, ST, 2 * D], fp16)
        WW = 2 * FT * H + HT * 2 * D
        work = sb("work", [P, WW], fp32)
        xs = sb("xs", [P, TPS, D], fp32)
        b2_row = sb("b2_row", [P, D], fp32)
        ident = sb("ident", [P, P], fp32)
        ones = sb("ones", [P, P], fp32)
        ones16 = sb("ones16", [P, P], fp16)
        b1T = sb("b1T", [P, HT], fp32)
        degree = sb("degree", [P, ST], fp32)
        rdegree = sb("rdegree", [P, ST], fp32)
        zmax = sb("zmax", [P, ST], fp32)
        amax = sb("amax", [P, 2], fp32)
        scale = sb("scale", [P, 4], fp32)
        srow = sb("srow", [1, 8], fp32)
        odd = sb("odd", [P, 1], fp32)
        frow = sb("frow", [1, 4], fp32)
        flag = sb("flag", [1, 1], i32)
        eps = sb("eps", [P, 1], fp32)
        stats = sb("stats", [P, TPS, 6], fp32)
        moments = sb("moments", [P, TPS, 2], fp32)
        deviation = sb("deviation", [P, TPS, 3], fp32)

        take = carve(work)
        iota_key = take(KEYS // 2, fp16)
        iota_src = take(P // 2, fp16)
        hot_key = take(2 * CH * KEYS // 2, fp16).rearrange("p (r c) -> p r c", c=KEYS)
        hot_src = take(2 * CH * P // 2, fp16).rearrange("p (r c) -> p r c", c=P)
        zero16 = take(P // 2, fp16)
        key_base = take(GS)
        group_base = take(NG)
        row_index = take(NG * RPC, u32)
        slot_key, slot_src = take(GS), take(GS)
        gathers = take(2 * EC)
        rows = gathers[:, 0:2 * P].rearrange("p (i k e) -> p i k e", k=2, e=ROW)
        unmixed = gathers[:, 2 * P:4 * P].rearrange("p (k e) -> p k e", k=2)
        all_keys, all_srcs = gathers[:, 0:EC], gathers[:, EC:2 * EC]
        take = carve(work)
        z_in = [take(XC * D).rearrange("p (t f) -> p t f", f=D) for _ in range(2)]
        y = take(TPS * D).rearrange("p (n f) -> p n f", f=D)

        def split_weights(words):
            return (words[:, 0:2 * FT * H].rearrange("p (k h) -> p k h", h=H),
                    words[:, 2 * FT * H:].rearrange("p (m o) -> p m o", o=2 * D))

        STRIP = ST * SB // 2
        weights_first = counts[:, 2 * STRIP * (NFULL - 1):2 * STRIP * (NFULL - 1) + 2 * WW].bitcast(fp32)
        weights_later = counts[:, 2 * STRIP:2 * STRIP + 2 * WW].bitcast(fp32)

        take = carve(counts[:, 2 * STRIP * 2:2 * STRIP * (NFULL - 1)].bitcast(fp32))
        x_in = take(ST * D).rearrange("p (t f) -> p t f", f=D)
        w1_in = take(2 * HT * D).rearrange("p (k m f) -> p k m f", k=2, f=D)
        w2_in = take(2 * FT * H).rearrange("p (k o h) -> p k o h", k=2, h=H)
        keys = take(2 * EC).rearrange("p (r k e) -> p r k e", k=2, e=ROW)
        pad_rows = take(2 * ROW)
        dst_i, dst_next, src_i = take(EC, i32), take(EC, i32), take(EC, i32)
        k_win, k_dst, k_tile, k_src, k_sum = (take(EC, i32) for _ in range(5))
        disorder = take(EC)
        first_dst = take(TR)
        window_start = take(NWIN + 1)
        starts_below = take(TR * ((NWIN + 2) // 2), fp16).rearrange("p (t w) -> p t w", t=TR)[:, :, 0:NWIN + 1]
        rows_below = take(NWIN + 1)
        first_row = take(NWIN)
        row_span = take(NWIN)
        slot_row = take(NG * GS)
        slot_in = take(NG * GS)
        quarter = take(NG * RPC)

        take = carve(counts[:, 0:ST * SB].bitcast(fp32))
        hT = take(HT * SB).rearrange("p (m c) -> p m c", c=SB)
        aggT = take(FT * SB).rearrange("p (k c) -> p k c", c=SB)
        xT = take(FT * SB).rearrange("p (k c) -> p k c", c=SB)
        inv_degree = take(SB)
        max_degree = take(SB)
        z_out = take(2 * D).rearrange("p (b f) -> p b f", b=2)

        bank = [ctx.enter_context(nc.psum_tensor(f"bank{i}", [P, 512], fp32))[:] for i in range(8)]

        def strip(s):
            return counts[:, bass.ds(s * (ST * SB), ST * SB)].rearrange("p (t c) -> p t c", c=SB)

        last_strip = counts[:, NFULL * ST * SB:].rearrange("p (t c) -> p t c", c=LASTW)

        def windows(bank_):
            return bank_[:, 0:KEYS].rearrange("p (t c) -> p t c", c=WIN)

        edges_in = sem("edges_in")
        next_in = sem("next_in")
        x_loaded = sem("x_loaded")
        w_in = sem("w_in")
        bias_in = sem("bias_in")
        b2_in = sem("b2_in")
        padded = sem("padded")
        consts = sem("consts")
        idents = sem("idents")
        prep = sem("prep")
        below_ready = sem("below_ready")
        rows_counted = sem("rows_counted")
        order_ready = sem("order_ready")
        order_summed = sem("order_summed")
        flag_ready = sem("flag_ready")
        keys_ready = sem("keys_ready")
        rows_stored = sem("rows_stored")
        slot_row_ready = sem("slot_row_ready")
        slot_row_turned = sem("slot_row_turned")
        index_ready = sem("index_ready")
        xmax_ready = sem("xmax_ready")
        max_turned = sem("max_turned")
        scale_row = sem("scale_row")
        scale_spread = sem("scale_spread")
        scale_ready = sem("scale_ready")
        high_ready = sem("high_ready")
        x_scaled = sem("x_scaled")
        low_ready = sem("low_ready")
        w_turned = sem("w_turned")
        w_copied = sem("w_copied")
        w_stored = sem("w_stored")
        w_back = sem("w_back")
        gathered = sem("gathered")
        rows_unmixed = sem("rows_unmixed")
        rows_turned = sem("rows_turned")
        slots_ready = sem("slots_ready")
        hot_ready = sem("hot_ready")
        window_summed = sem("window_summed")
        window_stored = sem("window_stored")
        early_out = [sem(f"early_out{i}") for i in range(2)]
        early_back = sem("early_back")
        all_in = sem("all_in")
        all_keyed = sem("all_keyed")
        all_hot = sem("all_hot")
        all_used = sem("all_used")
        all_summed = sem("all_summed")
        all_stored = sem("all_stored")
        xs_in = sem("xs_in")
        turned = sem("turned")
        turned_copied = sem("turned_copied")
        degree_summed = sem("degree_summed")
        agg_summed = sem("agg_summed")
        degree_ready = sem("degree_ready")
        inverse_ready = sem("inverse_ready")
        agg_ready = sem("agg_ready")
        h_summed = sem("h_summed")
        h_ready = sem("h_ready")
        zr_summed = sem("zr_summed")
        z_copied = sem("z_copied")
        r_added = sem("r_added")
        b2_added = sem("b2_added")
        z_stored = [sem(f"z_stored{b}") for b in range(2)]
        r_stored = sem("r_stored")
        z_loaded = [sem(f"z_loaded{b}") for b in range(2)]
        zmax_ready = sem("zmax_ready")
        rdegree_ready = sem("rdegree_ready")
        out_summed = sem("out_summed")
        res_in = [sem(f"res_in{n}") for n in range(TPS)]
        high_joined = sem("high_joined")
        bank_read = sem("bank_read")
        stats_ready = sem("stats_ready")
        moments_ready = sem("moments_ready")
        root_ready = sem("root_ready")
        root_inverted = sem("root_inverted")
        factors_ready = sem("factors_ready")
        normed = sem("normed")
        out_stored = [sem(f"out_stored{n}") for n in range(TPS)]

        NSPLIT = ST // XC
        MAIN = E - ETAIL
        TURNS = FT + 1
        QUARTER = SB // TPS
        WPQ = WPS // TPS
        SUMS, LATER, BUILD = "sums", "later", "build"
        AGG, HID, ZR, TURN = (0, 1), (0, 1), (3, 4), 5
        DEG, BUILT = 2, (6, 7)

        def layer_plan(s, built):
            if s == 0:
                pieces = [("Q", (TPS - 1, t), 0.27) for t in range(ST)] + [("E", 0, 0.0)]
                pieces += [("W!", 4, 0.0), ("F", 0, 0.0), ("G", 0, 0.2), ("X", 0, 1.2), ("W!", 3, 0.0)]
            else:
                pieces = [("D", t, 1.07) for t in range(0, ST, XC)] + [("E", 0, 0.0)]
                pieces += [("A", t, 0.86) for t in range(8)] + [("G", 0, 0.2)]
                pieces += [("A", t, 0.86) for t in range(8, 18)] + [("X", 0, 1.2)]
                pieces += [("A", t, 0.86) for t in range(18, ST)] + [("F", 0, 0.0), ("W!", 2, 0.0)]
            pieces += [("H", m, 3.5) for m in range(HT)]
            pieces += [("Z", n, 3.5) for n in range(TPS if s < NFULL else 1)]
            fixed = sum(n for what, n, _ in pieces if what == "W!")
            total = sum(time for _, _, time in pieces)
            free = max(built - fixed - 2, 0)
            plan, windows_, spent, spread = [], 0, 0.0, 0
            for what, n, time in pieces:
                if what == "W!":
                    for _ in range(n):
                        if windows_ < built:
                            plan.append(("W", windows_))
                            windows_ += 1
                    continue
                plan.append((what, n))
                spent += time
                while spread < free * spent / total - 1e-9 and windows_ < built:
                    plan.append(("W", windows_))
                    windows_ += 1
                    spread += 1
            if built == WPS and s + 2 < NG:
                plan.append(("R", 0))
            while windows_ < built:
                plan.append(("W", windows_))
                windows_ += 1
            return plan

        def first_plan():
            plan = [("W", k) for k in range(WPQ)]
            for q in range(TPS - 1):
                done = 0
                for k in range(WPQ):
                    plan.append(("W", (q + 1) * WPQ + k))
                    if q == TPS - 2 and k == WPQ - 3:
                        plan.append(("R", 0))
                    until = ST * (k + 1) // WPQ
                    plan += [("Q", (q, t)) for t in range(done, until)]
                    done = until
            return plan

        def windows_in(s):
            return 0 if s > NFULL else WLAST if s == NFULL else WPS

        def run_layers(engine, step, build):
            for s in (0, 1):
                step(s, layer_plan(s, windows_in(s + 1) if build else 0), s)
            with engine.Fori(2, NFULL - 1) as s:
                step(s, layer_plan(2, WPS if build else 0), 2)
            step(NFULL - 1, layer_plan(NFULL - 1, WLAST if build else 0), NFULL - 1)
            step(NFULL, layer_plan(NFULL, 0), NFULL)

        def tiles_of(kind):
            return (1, NLAST, NLAST) if kind == NFULL else (TPS, P, SB)

        def full_rows(ap, first=0):
            return ap[first:first + MAIN].rearrange("(p e) -> p e", e=EC)

        def tail_row(ap, first, n):
            return ap[first:first + n].rearrange("(p e) -> p e", p=1)

        LOOPED = (NFULL - 2) * TPS

        def tile_of(q):
            if q < LOOPED:
                return 2 + q // TPS, q % TPS, P
            if q == LOOPED:
                return NFULL, 0, NLAST
            return (q - LOOPED - 1) // TPS, (q - LOOPED - 1) % TPS, P

        block = ctx.enter_context(nc.Block())

        @block.sync
        def _(sp):
            sp.wait_ge(padded, 3)
            sp.dma_start(dst_i[0:EFULL, :], full_rows(dst)).then_inc(edges_in, 16)
            sp.dma_start(dst_i[EFULL:EFULL + 1, 0:ETAIL], tail_row(dst, MAIN, ETAIL)).then_inc(edges_in, 16)
            sp.dma_start(src_i[0:EFULL, :], full_rows(src)).then_inc(edges_in, 16)
            sp.dma_start(src_i[EFULL:EFULL + 1, 0:ETAIL], tail_row(src, MAIN, ETAIL)).then_inc(edges_in, 16)
            sp.dma_start(dst_next[0:EFULL, :], full_rows(dst, 1)).then_inc(next_in, 16)
            sp.dma_start(dst_next[EFULL:EFULL + 1, 0:ETAIL - 1],
                         tail_row(dst, MAIN + 1, ETAIL - 1)).then_inc(next_in, 16)
            sp.wait_ge(padded, 4)
            sp.dma_start(x_in[:, 0:ST - 1, :],
                         x[0:(ST - 1) * P, :].rearrange("(t p) f -> p t f", p=P)).then_inc(x_loaded, 16)
            sp.dma_start(x_in[0:NLAST, ST - 1, :], x[(ST - 1) * P:N, :]).then_inc(x_loaded, 16)
            sp.wait_ge(keys_ready, 2)
            sp.dma_start(rows_dram[0:NROWS, :].rearrange("(p r) c -> p (r c)", r=TR),
                         keys.rearrange("p r k e -> p (r k e)")).then_inc(rows_stored, 16)
            sp.dma_start(rows_dram[NROWS:NROWS + P, :], pad_rows).then_inc(rows_stored, 16)
            sp.dma_start(b2_row, b2l.partition_broadcast(P)).then_inc(b2_in, 16)
            sp.wait_ge(w_copied, 2 * FT + HT)
            sp.dma_start(wT_dram, weights_first).then_inc(w_stored, 16)

            def spill(s):
                sp.dma_start(early_dram[s], counts[:, 2 * STRIP * s:2 * STRIP * (s + 1)]).then_inc(early_out[s], 16)

            def steps(build):
                def step(s, plan, kind):
                    tiles, nodes, _ = tiles_of(kind)
                    if kind == 1 and build:
                        sp.wait_ge(window_stored, 2 * WPS)
                        spill(1)
                    if kind:
                        sp.wait_ge(r_stored, s * 16)
                    sp.dma_start(xs[0:nodes, 0:tiles, :],
                                 x[bass.ds(s * SB, nodes * tiles), :].rearrange("(n p) f -> p n f", p=nodes))\
                        .then_inc(xs_in, 16)
                    if kind == 1:
                        sp.wait_ge(early_out[1], 16)
                        sp.wait_ge(agg_summed, 2)
                        sp.wait_ge(w_stored, 16)
                        sp.dma_start(weights_later, wT_dram).then_inc(w_back, 16)
                    if kind == NFULL:
                        prefetch_z(build)
                    for n in range(tiles):
                        sp.wait_ge(z_copied, s * TPS + n + 1)
                        sp.dma_start(zr_dram[bass.ds(s * SB + n * P, nodes), 0:D], z_out[0:nodes, n % 2, :])\
                            .then_inc(z_stored[n % 2], 16)
                    sp.wait_ge(r_added, s * TPS + tiles)
                    sp.dma_start(zr_dram[bass.ds(s * SB, nodes * tiles), D:2 * D]
                                 .rearrange("(n p) f -> p n f", p=nodes), xs[0:nodes, 0:tiles, :]).then_inc(r_stored, 16)
                run_layers(sp, step, build)

            def load_z(c):
                full = XC if c < NSPLIT - 1 else XC - 1
                sp.dma_start(z_in[c % 2][:, 0:full, :],
                             zr_dram[c * XC * P:(c * XC + full) * P, 0:D].rearrange("(t p) f -> p t f", p=P))\
                    .then_inc(z_loaded[c % 2], 16)
                if full < XC:
                    sp.dma_start(z_in[c % 2][0:NLAST, full, :], zr_dram[(ST - 1) * P:N, 0:D])\
                        .then_inc(z_loaded[c % 2], 16)

            def prefetch_z(build):
                if build:
                    sp.wait_ge(window_stored, NWIN)
                for b in range(2):
                    sp.wait_ge(z_stored[b], 16 * NFULL * TPS // 2)
                load_z(0)
                load_z(1)

            sp.wait_ge(flag_ready, 1)
            slow = sp.value_load(flag[0:1, 0:1])
            with sp.If(slow > 0):
                sp.wait_ge(rows_stored, 32)
                back = rows_dram[0:NROWS, :].rearrange("(p r) (k e) -> p r k e", r=TR, k=2)
                sp.dma_start(all_keys.rearrange("p (r e) -> p r e", e=ROW), back[:, :, 0, :]).then_inc(all_in, 16)
                sp.dma_start(all_srcs.rearrange("p (r e) -> p r e", e=ROW), back[:, :, 1, :]).then_inc(all_in, 16)
                sp.wait_ge(w_stored, 16)
                sp.wait_ge(all_stored, NWIN)
                sp.wait_ge(all_keyed, NWIN)
                sp.dma_start(work, wT_dram).then_inc(w_back, 16)
                spill(0)
                spill(1)
                steps(False)
            with sp.Else():
                sp.wait_ge(window_stored, WPS)
                spill(0)
                steps(True)

            sp.wait_ge(z_stored[0], 16 * (NFULL * TPS // 2 + 1))
            for c in range(2, NSPLIT):
                sp.wait_ge(low_ready, NSPLIT + c - 1)
                load_z(c)
            sp.wait_ge(zr_summed, NFULL * TPS + 1)
            sp.dma_start(counts[:, 0:4 * STRIP].rearrange("p (s c) -> p s c", s=2),
                         early_dram.rearrange("s p c -> p s c")).then_inc(early_back, 16)

            def load_res(t, n, nodes):
                sp.dma_start(y[0:nodes, n, :], zr_dram[bass.ds(t * P, nodes), D:2 * D]).then_inc(res_in[n], 16)

            def store_out(q, t, n, nodes):
                sp.wait_ge(normed, q + 1)
                sp.dma_start(out[bass.ds(t * P, nodes), :], y[0:nodes, n, :]).then_inc(out_stored[n], 16)

            sp.wait_ge(r_stored, 16 * NG)
            for n in range(TPS):
                load_res(2 * TPS + n, n, P)
            with sp.Fori(1, NFULL - 2) as g:
                for n in range(TPS):
                    store_out((g - 1) * TPS + n, (g + 1) * TPS + n, n, P)
                    sp.wait_ge(out_stored[n], g * 16)
                    load_res((g + 2) * TPS + n, n, P)
            for q in range(LOOPED - TPS, ST):
                s, n, nodes = tile_of(q)
                store_out(q, s * TPS + n, q % TPS, nodes)
                if q + TPS < ST:
                    s, n, nodes = tile_of(q + TPS)
                    sp.wait_ge(out_stored[q % TPS], 16 * (q // TPS + 1))
                    load_res(s * TPS + n, q % TPS, nodes)
            for n in range(TPS):
                sp.wait_ge(out_stored[n], 16 * len(range(n, ST, TPS)))

        @block.gpsimd
        def _(pool):
            G = nc.gpsimd
            G.memset(dst_i, FAR).then_inc(padded, 1)
            G.memset(dst_next, FAR).then_inc(padded, 1)
            G.memset(src_i, 0).then_inc(padded, 1)
            G.memset(x_in[:, ST - 1, :], 0.0).then_inc(padded, 1)

            def ramp(where, pattern):
                G.iota(where, pattern, base=0, channel_multiplier=0,
                       allow_small_or_imprecise_dtypes=True).then_inc(consts, 1)

            ramp(window_start, [[WIN, NWIN + 1]])
            G.memset(ones16, 1.0).then_inc(consts, 1)
            G.memset(ones, 1.0).then_inc(consts, 1)
            G.memset(ident, 0.0).then_inc(idents, 1)
            pool.wait_ge(idents, 1)
            G.affine_select(out=ident, in_=ident, compare_op=ALU.not_equal, fill=1.0, base=0,
                            pattern=[[-1, P]], channel_multiplier=1).then_inc(consts, 1)
            ramp(slot_in[0:1, :], [[0, NG * WPS], [RPC, CH]])
            ramp(quarter, [[0, NG], [1, RPC]])
            ramp(key_base, [[STEP, WPS], [0, CH]])
            ramp(group_base, [[-STEP * WPS, NG]])
            ramp(iota_key, [[1, KEYS]])
            ramp(iota_src, [[1, P]])
            G.memset(zero16, 0.0).then_inc(consts, 1)

            def low_parts():
                for c in range(NSPLIT):
                    value, tiles = x_in[:, c * XC:(c + 1) * XC, :], slice(c * XC, (c + 1) * XC)
                    pool.wait_ge(high_ready, c + 1)
                    G.tensor_scalar(value, value, scale[:, 0:1], None, ALU.mult).then_inc(x_scaled, 1)
                    pool.wait_ge(x_scaled, c + 1)
                    G.tensor_tensor(parts[:, tiles, D:2 * D], value, parts[:, tiles, 0:D], ALU.subtract)\
                        .then_inc(low_ready, 1)

            def gather(g):
                if g >= 1:
                    pool.wait_ge(rows_unmixed, g)
                for i in range(RPC):
                    G.indirect_dma_start(
                        rows[0:GS, i].rearrange("p k e -> p (k e)"), None, rows_dram,
                        bass.IndirectOffsetOnAxis(row_index[0:GS, g * RPC + i:g * RPC + i + 1], 0))\
                        .then_inc(gathered, 16)

            def add_b2(s):
                tiles, nodes, _ = tiles_of(s)
                pool.wait_ge(turned, s * TURNS + TURNS)
                b2 = b2_row[0:nodes, :].rearrange("p (o f) -> p o f", o=1).broadcast_to([nodes, tiles, D])
                G.tensor_tensor(xs[0:nodes, 0:tiles, :], xs[0:nodes, 0:tiles, :], b2, ALU.add).then_inc(b2_added, 1)

            pool.wait_ge(flag_ready, 1)
            pool.wait_ge(b2_in, 16)
            slow = pool.value_load(flag[0:1, 0:1])
            with pool.If(slow > 0):
                low_parts()
                for s in range(NG):
                    add_b2(s)
            with pool.Else():
                pool.wait_ge(rows_stored, 32)
                pool.wait_ge(index_ready, 1)
                gather(0)
                gather(1)
                low_parts()
                gather(2)
                for s in range(NG):
                    if s + 3 < NG:
                        gather(s + 3)
                    add_b2(s)

        @block.vector
        def _(dve):
            V = nc.vector
            steps = [0]

            def then(ins):
                ins.then_inc(prep, 1)
                steps[0] += 1
                dve.wait_ge(prep, steps[0])

            def find_scale(which):
                dve.wait_ge(max_turned, which + 1)
                then(V.tensor_reduce(srow[0:1, 0:1], bank[DEG][0:1, 0:P], AX.X, ALU.max))
                then(V.tensor_scalar(srow[0:1, 1:2], srow[0:1, 0:1], TINY, None, ALU.max))
                then(V.tensor_scalar(srow[0:1, 2:3].bitcast(i32), srow[0:1, 1:2].bitcast(i32), EXP_MASK, None,
                                     ALU.bitwise_and))
                V.tensor_scalar(srow[0:1, 3:4].bitcast(i32), srow[0:1, 2:3].bitcast(i32), -1.0, EXP_SUM,
                                ALU.mult, ALU.add).then_inc(scale_row, 1)
                dve.wait_ge(scale_spread, which + 1)
                then(V.tensor_copy(scale[:, which:which + 1], bank[DEG][:, 256:257]))
                V.reciprocal(scale[:, 2 + which:3 + which], scale[:, which:which + 1]).then_inc(scale_ready, 1)

            V.memset(eps, EPS)
            V.memset(zmax, 0.0)
            V.memset(degree, 1.0)
            V.memset(pad_rows, -1.0).then_inc(keys_ready, 1)
            dve.wait_ge(edges_in, 4 * 16)
            then(V.tensor_copy(first_dst, dst_i[:, 0:EC:ROW]))
            dve.wait_ge(consts, 1)
            for t in range(TR):
                ins = V.tensor_scalar(starts_below[:, t, :], window_start, first_dst[:, t:t + 1], None, ALU.is_gt)
            ins.then_inc(below_ready, 1)
            V.tensor_scalar(k_win, dst_i, WIN.bit_length() - 1, STEP.bit_length() - 1,
                            ALU.arith_shift_right, ALU.logical_shift_left)
            V.tensor_scalar(k_dst, dst_i, WIN - 1, None, ALU.bitwise_and)
            V.tensor_scalar(k_tile, src_i, P.bit_length() - 1, WIN.bit_length() - 1,
                            ALU.arith_shift_right, ALU.logical_shift_left)
            then(V.tensor_scalar(k_src, src_i, P - 1, None, ALU.bitwise_and))
            then(V.tensor_tensor(k_sum, k_win, k_dst, ALU.add))
            V.tensor_tensor(keys[:, :, 0, :], k_sum.rearrange("p (r e) -> p r e", e=ROW),
                            k_tile.rearrange("p (r e) -> p r e", e=ROW), ALU.add)
            V.tensor_copy(keys[:, :, 1, :], k_src.rearrange("p (r e) -> p r e", e=ROW)).then_inc(keys_ready, 1)
            dve.wait_ge(rows_counted, 1)
            then(V.tensor_copy(rows_below[0:1, :], bank[DEG][0:1, 0:NWIN + 1]))
            then(V.tensor_scalar(first_row[0:1, :], rows_below[0:1, 0:NWIN], -1.0, 0.0, ALU.add, ALU.max))
            V.memset(slot_row[0:1, NWIN * CH:], 0.0)
            dve.wait_ge(consts, 6)
            first3 = first_row[0:1, :].rearrange("p (w o) -> p w o", o=1).broadcast_to([1, NWIN, CH])
            V.tensor_tensor(slot_row[0:1, 0:NWIN * CH].rearrange("p (w c) -> p w c", c=CH), first3,
                            slot_in[0:1, 0:NWIN * CH].rearrange("p (w c) -> p w c", c=CH), ALU.add)\
                .then_inc(slot_row_ready, 1)
            dve.wait_ge(next_in, 32)
            then(V.tensor_tensor(disorder, dst_i, dst_next, ALU.is_gt))
            V.tensor_reduce(odd, disorder, AX.X, ALU.add).then_inc(order_ready, 1)
            then(V.tensor_tensor(row_span[0:1, :], rows_below[0:1, 1:], first_row[0:1, :], ALU.subtract))
            then(V.tensor_reduce(frow[0:1, 0:1], row_span[0:1, :], AX.X, ALU.max))
            then(V.tensor_scalar(frow[0:1, 1:2], frow[0:1, 0:1], float(CAP), None, ALU.is_gt))
            dve.wait_ge(slot_row_turned, 1)
            V.tensor_tensor(row_index[0:GS, :], bank[DEG][0:GS, 320:320 + NG * RPC], quarter[0:GS, :],
                            ALU.add).then_inc(index_ready, 1)
            dve.wait_ge(order_summed, 1)
            V.tensor_tensor(flag, frow[0:1, 1:2], bank[DEG][0:1, 256:257], ALU.add).then_inc(flag_ready, 1)

            dve.wait_ge(x_loaded, 32)
            V.tensor_reduce(amax[:, 0:1], x_in.rearrange("p t f -> p (t f)"), AX.X, ALU.max,
                            apply_absolute_value=True).then_inc(xmax_ready, 1)
            find_scale(0)

            def take_slots(g, first=False):
                if not first:
                    dve.wait_ge(hot_ready, g * GS)
                dve.wait_ge(rows_turned, g + 1)
                V.scalar_tensor_tensor(out=slot_key, in0=bank[TURN][:, 0:GS], scalar=group_base[:, bass.ds(g, 1)],
                                       in1=key_base, op0=ALU.add, op1=ALU.subtract)
                V.tensor_copy(slot_src, bank[TURN][:, P:P + GS]).then_inc(slots_ready, 1)
                dve.wait_ge(slots_ready, g + 1)

            def window_hots(b, k, first=False):
                if not first:
                    dve.wait_ge(window_summed, b * WPS + (k - 1))
                for j in range(CH):
                    r = (k % 2) * CH + j
                    V.tensor_scalar(hot_key[:, r, :], iota_key, slot_key[:, k * CH + j:k * CH + j + 1],
                                    None, ALU.is_equal)
                    V.tensor_scalar(hot_src[:, r, :], iota_src, slot_src[:, k * CH + j:k * CH + j + 1],
                                    None, ALU.is_equal).then_inc(hot_ready, 1)

            def take_degrees(s, kind):
                cols = tiles_of(kind)[2]
                dve.wait_ge(degree_summed, s + 1)
                if kind == 0:
                    dve.wait_ge(agg_summed, 1)
                    dve.wait_ge(early_out[0], 16)
                else:
                    dve.wait_ge(turned, s * TURNS)
                V.tensor_scalar(max_degree[:, 0:cols], bank[DEG][:, 0:cols], 1.0, None, ALU.max)\
                    .then_inc(degree_ready, 1)
                dve.wait_ge(degree_ready, s + 1)
                V.reciprocal(inv_degree[:, 0:cols], max_degree[:, 0:cols]).then_inc(inverse_ready, 1)
                dve.wait_ge(inverse_ready, s + 1)

            def take_sums(s, kind):
                cols = tiles_of(kind)[2]
                dve.wait_ge(agg_summed, s + 1)
                if kind:
                    dve.wait_ge(h_summed, s * HT)
                for k in range(FT):
                    V.scalar_tensor_tensor(out=aggT[:, k, 0:cols], in0=bank[AGG[k]][:, 0:cols], scalar=scale[:, 2:3],
                                           in1=inv_degree[:, 0:cols], op0=ALU.mult, op1=ALU.mult)\
                        .then_inc(agg_ready, 1)

            def take_outputs(s, kind, n):
                nodes = tiles_of(kind)[1]
                b = bank[ZR[n % 2]]
                if n == 0:
                    dve.wait_ge(b2_added, s + 1)
                dve.wait_ge(z_copied, s * TPS + n + 1)
                V.tensor_reduce(zmax[0:nodes, bass.ds(s * TPS + n, 1)], b[0:nodes, 0:D], AX.X, ALU.max,
                                apply_absolute_value=True)
                V.tensor_tensor(xs[0:nodes, n, :], b[0:nodes, D:2 * D], xs[0:nodes, n, :], ALU.add)\
                    .then_inc(r_added, 1)

            def follow(s, plan, kind, b):
                windows_ = sum(what == "W" for what, _ in plan)
                made = passed = 0
                for what, n in plan:
                    if what == "W":
                        passed += 1
                    if what in "EFZ":
                        while made < min(passed + 2, windows_):
                            window_hots(b, made)
                            made += 1
                        if what == "E" and kind:
                            take_degrees(s, kind)
                        elif what == "E":
                            continue
                        elif what == "F":
                            if kind == 0:
                                take_degrees(s, kind)
                            take_sums(s, kind)
                        else:
                            take_outputs(s, kind, n)
                while made < windows_:
                    window_hots(b, made)
                    made += 1
                if any(what == "R" for what, _ in plan):
                    take_slots(s + 2)

            def steps_of(build):
                run_layers(dve, lambda s, plan, kind: follow(s, plan, kind, s + 1), build)

            dve.wait_ge(consts, 11)
            slow = dve.value_load(flag[0:1, 0:1])
            with dve.If(slow > 0):
                dve.wait_ge(all_in, 32)
                with dve.Fori(0, NWIN) as w:
                    with dve.Fori(0, EC // 4) as c:
                        dve.wait_ge(all_used, w * (EC // 4) + c + 1)
                        for j in range(4):
                            V.tensor_scalar(hot_key[:, j, :], iota_key, all_keys[:, bass.ds(c * 4 + j, 1)], None,
                                            ALU.is_equal)
                            ins = V.tensor_scalar(hot_src[:, j, :], iota_src, all_srcs[:, bass.ds(c * 4 + j, 1)],
                                                  None, ALU.is_equal)
                        ins.then_inc(all_hot, 1)
                    dve.wait_ge(all_hot, w * (EC // 4) + EC // 4)
                    V.tensor_scalar(all_keys, all_keys, float(-STEP), None, ALU.add).then_inc(all_keyed, 1)
                    dve.wait_ge(all_keyed, w + 1)
                steps_of(False)
            with dve.Else():
                take_slots(0, True)
                for k in range(WPS):
                    window_hots(0, k, k < 2)
                take_slots(1)
                steps_of(True)

            def low_part(value, nodes, t0, n, which):
                return V.scalar_tensor_tensor(
                    out=parts[0:nodes, t0:t0 + n, D:2 * D], in0=value, scalar=scale[0:nodes, which:which + 1],
                    in1=parts[0:nodes, t0:t0 + n, 0:D], op0=ALU.mult, op1=ALU.subtract)

            dve.wait_ge(r_added, NFULL * TPS + 1)
            V.tensor_reduce(amax[:, 1:2], zmax, AX.X, ALU.max).then_inc(zmax_ready, 1)
            find_scale(1)
            dve.wait_ge(scale_ready, 2)
            for c in range(NSPLIT):
                dve.wait_ge(high_ready, NSPLIT + c + 1)
                if c < NSPLIT - 1:
                    low_part(z_in[c % 2], P, c * XC, XC, 1).then_inc(low_ready, 1)
                else:
                    low_part(z_in[c % 2][:, 0:XC - 1, :], P, c * XC, XC - 1, 1)
                    low_part(z_in[c % 2][0:NLAST, XC - 1:XC, :], NLAST, ST - 1, 1, 1).then_inc(low_ready, 1)
            dve.wait_ge(turned_copied, NG * TURNS)
            then(V.reciprocal(rdegree, degree))
            V.tensor_scalar(rdegree, rdegree, scale[:, 3:4], None, ALU.mult).then_inc(rdegree_ready, 1)
            dve.wait_ge(rdegree_ready, 1)

            def join(q, t, n, nodes, loads, b):
                row = y[0:nodes, n, :]
                dve.wait_ge(out_summed, q + 1)
                dve.wait_ge(res_in[n], loads)
                V.scalar_tensor_tensor(out=row, in0=b[0:nodes, 0:D], scalar=rdegree[0:nodes, bass.ds(t, 1)],
                                       in1=row, op0=ALU.mult, op1=ALU.add).then_inc(high_joined, 1)
                dve.wait_ge(high_joined, q + 1)
                V.scalar_tensor_tensor(out=row, in0=b[0:nodes, D:2 * D], scalar=rdegree[0:nodes, bass.ds(t, 1)],
                                       in1=row, op0=ALU.mult, op1=ALU.add).then_inc(bank_read, 1)
                dve.wait_ge(bank_read, q + 1)
                V.bn_stats(stats[0:nodes, n, :], row).then_inc(stats_ready, 1)

            def root(q, n, nodes):
                dve.wait_ge(root_ready, q + 1)
                V.reciprocal(deviation[0:nodes, n, 1:2], deviation[0:nodes, n, 0:1]).then_inc(root_inverted, 1)

            def aggregate_stats(n, nodes):
                V.bn_aggr(moments[0:nodes, n, :], stats[0:nodes, n, :]).then_inc(moments_ready, 1)

            def factor(q, n, nodes):
                dve.wait_ge(root_inverted, q + 1)
                V.scalar_tensor_tensor(out=deviation[0:nodes, n, 2:3], in0=moments[0:nodes, n, 0:1], scalar=-1.0,
                                       in1=deviation[0:nodes, n, 1:2], op0=ALU.mult, op1=ALU.mult)\
                    .then_inc(factors_ready, 1)

            def finish(q, t, n, nodes, loads, b, before=P):
                join(q, t, n, nodes, loads, b)
                dve.wait_ge(stats_ready, q + 1)
                root(q - 1, (n - 1) % TPS, before)
                aggregate_stats(n, nodes)
                factor(q - 1, (n - 1) % TPS, before)

            join(0, 2 * TPS, 0, P, 16, bank[0])
            dve.wait_ge(stats_ready, 1)
            aggregate_stats(0, P)
            for q in range(1, 2 * TPS):
                finish(q, 2 * TPS + q, q % TPS, P, 16 * (q // TPS + 1), bank[q])
            with dve.Fori(2, NFULL - 2) as g:
                for n in range(TPS):
                    finish(g * TPS + n, (g + 2) * TPS + n, n, P, g * 16 + 16, bank[n])
            for q in range(LOOPED, ST):
                s, n, nodes = tile_of(q)
                finish(q, s * TPS + n, q % TPS, nodes, 16 * (q // TPS + 1), bank[TPS + q % TPS], tile_of(q - 1)[2])
            root(ST - 1, (ST - 1) % TPS, P)
            factor(ST - 1, (ST - 1) % TPS, P)

        @block.scalar
        def _(act):
            A = nc.scalar
            act.wait_ge(edges_in, 4 * 16)
            act.dma_start(w1_in[:, 0], w1l.rearrange("(m p) f -> p m f", p=P)).then_inc(w_in, 16)
            act.dma_start(w1_in[:, 1], w1r.rearrange("(m p) f -> p m f", p=P)).then_inc(w_in, 16)
            act.dma_start(w2_in[:, 0], w2l.rearrange("(o p) h -> p o h", p=P)).then_inc(w_in, 16)
            act.dma_start(w2_in[:, 1], w2r.rearrange("(o p) h -> p o h", p=P)).then_inc(w_in, 16)
            act.dma_start(b1T, b1l.rearrange("(m p) -> p m", p=P), allow_slow_non_contiguous=True).then_inc(bias_in, 16)

            def high_part(value, nodes, t0, n, which):
                return A.activation(parts[0:nodes, t0:t0 + n, 0:D], value, ACT.Copy,
                                    scale=scale[0:nodes, which:which + 1])

            act.wait_ge(scale_ready, 1)
            for c in range(NSPLIT):
                high_part(x_in[:, c * XC:(c + 1) * XC, :], P, c * XC, XC, 0).then_inc(high_ready, 1)

            def unmix(g):
                act.wait_ge(gathered, (g * RPC + RPC) * 16)
                A.copy(unmixed[0:GS].rearrange("p k (i e) -> p k i e", e=ROW),
                       rows[0:GS].rearrange("p i k e -> p k i e")).then_inc(rows_unmixed, 1)

            def copy_weights():
                w1T, w2T = split_weights(weights_first)
                for k in range(2 * FT + HT):
                    act.wait_ge(w_turned, k + 1)
                    to = w1T[:, k, :] if k < 2 * FT else w2T[:, k - 2 * FT, :]
                    A.copy(to, bank[ZR[k % 2]]).then_inc(w_copied, 1)

            def store_window(where, w, b, done, summed, stored):
                act.wait_ge(summed, done + 1)
                A.copy(where[:, :, bass.ds(w * WIN, WIN)], windows(bank[BUILT[b]])).then_inc(stored, 1)

            def follow(s, plan, kind, b):
                tiles, nodes, cols = tiles_of(kind)
                where = None if kind >= NFULL else last_strip if kind == NFULL - 1 else strip(b)
                for what, n in plan:
                    if what == "W":
                        store_window(where, n, n % 2, b * WPS + n, window_summed, window_stored)
                    elif what == "G":
                        act.wait_ge(turned, s * TURNS + 1)
                        A.copy(degree[0:nodes, bass.ds(s * TPS, tiles)], bank[TURN][0:nodes, 0:tiles])\
                            .then_inc(turned_copied, 1)
                        if any(x == "R" for x, _ in plan):
                            unmix_next(s)
                    elif what == "X":
                        for k in range(FT):
                            act.wait_ge(turned, s * TURNS + k + 2)
                            A.copy(xT[:, k, 0:cols], bank[TURN][:, 0:cols]).then_inc(turned_copied, 1)
                    elif what == "H":
                        if kind and n == 0:
                            act.wait_ge(zr_summed, s * TPS)
                        act.wait_ge(h_summed, s * HT + n + 1)
                        A.activation(hT[:, n, 0:cols], bank[HID[n % 2]][:, 0:cols], ACT.Relu, bias=b1T[:, n:n + 1])\
                            .then_inc(h_ready, 1)
                    elif what == "Z":
                        act.wait_ge(zr_summed, s * TPS + n + 1)
                        if kind:
                            act.wait_ge(z_stored[n % 2], s * (16 * TPS // 2) + 16 * (n // 2))
                        elif n >= 2:
                            act.wait_ge(z_stored[n % 2], 16 * (n // 2))
                        A.copy(z_out[0:nodes, n % 2, :], bank[ZR[n % 2]][0:nodes, 0:D]).then_inc(z_copied, 1)

            def unmix_next(s):
                act.wait_ge(rows_turned, s + 2)
                unmix(s + 2)

            def steps_of(build):
                run_layers(act, lambda s, plan, kind: follow(s, plan, kind, s + 1), build)

            slow = act.value_load(flag[0:1, 0:1])
            with act.If(slow > 0):
                copy_weights()
                with act.Fori(0, NFULL) as s:
                    with act.Fori(0, WPS) as w:
                        store_window(strip(s), w, 0, s * WPS + w, all_summed, all_stored)
                with act.Fori(0, WLAST) as w:
                    store_window(last_strip, w, 0, w + NFULL * WPS, all_summed, all_stored)
                act.wait_ge(bias_in, 16)
                steps_of(False)
            with act.Else():
                unmix(0)
                copy_weights()
                act.wait_ge(rows_turned, 1)
                unmix(1)
                for what, n in first_plan():
                    if what == "W":
                        store_window(strip(0), n, n % 2, n, window_summed, window_stored)
                act.wait_ge(bias_in, 16)
                steps_of(True)

            act.wait_ge(scale_ready, 2)
            for c in range(NSPLIT):
                if c < NSPLIT - 1:
                    act.wait_ge(z_loaded[c % 2], 16 * (c // 2 + 1))
                    high_part(z_in[c % 2], P, c * XC, XC, 1).then_inc(high_ready, 1)
                else:
                    act.wait_ge(z_loaded[c % 2], 16 * (c // 2 + 2))
                    high_part(z_in[c % 2][:, 0:XC - 1, :], P, c * XC, XC - 1, 1)
                    high_part(z_in[c % 2][0:NLAST, XC - 1:XC, :], NLAST, ST - 1, 1, 1).then_inc(high_ready, 1)

            def norm(q, n, nodes):
                act.wait_ge(moments_ready, q + 1)
                A.activation(deviation[0:nodes, n, 0:1], moments[0:nodes, n, 1:2], ACT.Sqrt, bias=eps[0:nodes, :])\
                    .then_inc(root_ready, 1)
                act.wait_ge(factors_ready, q + 1)
                A.activation(y[0:nodes, n, :], y[0:nodes, n, :], ACT.Identity, scale=deviation[0:nodes, n, 1:2],
                             bias=deviation[0:nodes, n, 2:3]).then_inc(normed, 1)

            with act.Fori(0, NFULL - 2) as g:
                for n in range(TPS):
                    norm(g * TPS + n, n, P)
            for q in range(LOOPED, ST):
                norm(q, q % TPS, tile_of(q)[2])

        @block.tensor
        def _(pe):
            T = nc.tensor

            def mm(o, a, b, start=True, stop=True):
                return T.matmul(o, a, b, start=start, stop=stop)

            pe.wait_ge(consts, 4)
            pe.wait_ge(below_ready, 1)
            for t in range(TR):
                ins = mm(bank[DEG][0:1, 0:NWIN + 1], ones16[:, 0:1], starts_below[:, t, :], t == 0, t == TR - 1)
            ins.then_inc(rows_counted, 1)
            pe.wait_ge(slot_row_ready, 1)
            for g in range(NG):
                ins = mm(bank[DEG][0:GS, 320 + g * RPC:320 + (g + 1) * RPC], slot_row[0:1, g * GS:(g + 1) * GS],
                         ones[0:1, 0:RPC])
            ins.then_inc(slot_row_turned, 1)
            pe.wait_ge(order_ready, 1)
            pe.wait_ge(index_ready, 1)
            mm(bank[DEG][0:1, 256:257], odd, ones[:, 0:1]).then_inc(order_summed, 1)

            def spread_scale(which):
                T.transpose(bank[DEG][0:1, 0:P], amax[:, which:which + 1], ident).then_inc(max_turned, 1)
                pe.wait_ge(scale_row, which + 1)
                mm(bank[DEG][:, 256:257], ones[0:1, :], srow[0:1, 3:4]).then_inc(scale_spread, 1)

            pe.wait_ge(xmax_ready, 1)
            spread_scale(0)

            def turn_weights():
                pe.wait_ge(w_in, 4 * 16)
                for k in range(2 * FT + HT):
                    if k >= 2:
                        pe.wait_ge(w_copied, k - 1)
                    for i in range(4):
                        if k < 2 * FT:
                            tile = w1_in[:, k // FT, i, (k % FT) * P:(k % FT + 1) * P]
                        else:
                            tile = w2_in[:, i // FT, i % FT, (k - 2 * FT) * P:(k - 2 * FT + 1) * P]
                        ins = T.transpose(bank[ZR[k % 2]][:, i * P:(i + 1) * P], tile, ident)
                    ins.then_inc(w_turned, 1)

            def turn_rows(g):
                pe.wait_ge(rows_unmixed, g + 1)
                for k in range(2):
                    ins = T.transpose(bank[TURN][:, k * P:k * P + GS], unmixed[0:GS, k, :], ident[0:GS, 0:GS])
                ins.then_inc(rows_turned, 1)

            def sum_window(b, k):
                if not (isinstance(b, int) and b == 0 and k < 2):
                    pe.wait_ge(window_stored, b * WPS + (k - 1))
                for j in range(CH):
                    pe.wait_ge(hot_ready, b * GS + (k * CH + j + 1))
                    r = (k % 2) * CH + j
                    ins = mm(bank[BUILT[k % 2]][:, 0:KEYS], hot_src[:, r, :], hot_key[:, r, :], j == 0, j == CH - 1)
                ins.then_inc(window_summed, 1)

            def sum_degrees(where, t, a, cols):
                return mm(bank[DEG][:, a:a + cols], ones16, where[:, t, a:a + cols], t == 0, t == ST - 1)

            def sum_tile(where, t, a, cols):
                for k in range(FT):
                    for part in range(2):
                        c = part * D + k * P
                        ins = mm(bank[AGG[k]][:, a:a + cols], parts[:, t, c:c + P], where[:, t, a:a + cols],
                                 t == 0 and part == 0, t == ST - 1 and part == 1)
                return ins

            def sum_quarter(q, t, built):
                if t == 0 and built:
                    pe.wait_ge(window_stored, (q + 1) * WPQ)
                if q == 0 and t % XC == 0:
                    pe.wait_ge(low_ready, t // XC + 1)
                by_degree = sum_degrees(strip(0), t, q * QUARTER, QUARTER)
                by_tile = sum_tile(strip(0), t, q * QUARTER, QUARTER)
                if q == TPS - 1 and t == ST - 1:
                    by_degree.then_inc(degree_summed, 1)
                    by_tile.then_inc(agg_summed, 1)

            def follow(s, plan, kind, b, build, weights_):
                tiles, nodes, cols = tiles_of(kind)
                where = last_strip if kind == NFULL else strip(s)
                w1T, w2T = split_weights(weights_)
                for what, n in plan:
                    if what == "W":
                        sum_window(b, n)
                    elif what == "R":
                        pe.wait_ge(turned_copied, s * TURNS + TURNS)
                        turn_rows(s + 2)
                    elif what == "Q":
                        sum_quarter(*n, build)
                    elif what == "D":
                        if n == 0:
                            if build:
                                pe.wait_ge(window_stored, NWIN if kind == NFULL else s * WPS + WPS)
                            pe.wait_ge(degree_ready, s)
                        for t in range(n, n + XC):
                            ins = sum_degrees(where, t, 0, cols)
                        if t == ST - 1:
                            ins.then_inc(degree_summed, 1)
                    elif what == "A":
                        if n == 0:
                            pe.wait_ge(h_ready, s * HT)
                        ins = sum_tile(where, n, 0, cols)
                        if n == ST - 1:
                            ins.then_inc(agg_summed, 1)
                    elif what == "G":
                        pe.wait_ge(degree_ready, s + 1)
                        if build and kind < NFULL:
                            pe.wait_ge(slots_ready, s + 2)
                        elif build:
                            pe.wait_ge(slots_ready, NG)
                        if kind:
                            pe.wait_ge(turned_copied, s * TURNS)
                        for i in range(tiles):
                            ins = mm(bank[TURN][0:nodes, i:i + 1], max_degree[0:1, i * P:i * P + nodes], ones[0:1, 0:1])
                        ins.then_inc(turned, 1)
                    elif what == "X":
                        pe.wait_ge(xs_in, s * 16 + 16)
                        for k in range(FT):
                            pe.wait_ge(turned_copied, s * TURNS + k + 1)
                            for i in range(tiles):
                                ins = T.transpose(bank[TURN][:, i * P:i * P + nodes],
                                                  xs[0:nodes, i, k * P:(k + 1) * P], ident[0:nodes, 0:nodes])
                            ins.then_inc(turned, 1)
                    elif what == "H":
                        if n == 0:
                            pe.wait_ge(agg_ready, s * FT + FT)
                            pe.wait_ge(turned_copied, s * TURNS + TURNS)
                        else:
                            if n >= 2:
                                pe.wait_ge(h_ready, s * HT + (n - 1))
                        for k in range(2 * FT):
                            operand = aggT[:, k, 0:cols] if k < FT else xT[:, k - FT, 0:cols]
                            ins = mm(bank[HID[n % 2]][:, 0:cols], w1T[:, k, n * P:(n + 1) * P], operand,
                                     k == 0, k == 2 * FT - 1)
                        ins.then_inc(h_summed, 1)
                    elif what == "Z":
                        if n == 0:
                            pe.wait_ge(h_ready, s * HT + HT)
                        if kind or n >= 2:
                            pe.wait_ge(r_added, s * TPS + (n - 1))
                        for m in range(HT):
                            ins = mm(bank[ZR[n % 2]][0:nodes, :], hT[:, m, n * P:n * P + nodes], w2T[:, m, :],
                                     m == 0, m == HT - 1)
                        ins.then_inc(zr_summed, 1)

            def steps_of(build):
                def step(s, plan, kind):
                    if kind == 2:
                        pe.wait_ge(w_back, 16 if build else 32)
                    follow(s, plan, kind, s + 1, build,
                           weights_later if kind >= 2 else weights_first if build else work)
                run_layers(pe, step, build)

            slow = pe.value_load(flag[0:1, 0:1])
            with pe.If(slow > 0):
                turn_weights()
                one = bank[BUILT[0]][:, 0:KEYS]
                mm(one, zero16, iota_key).then_inc(all_used, 1)
                with pe.Fori(0, NWIN) as w:
                    mm(one, zero16, iota_key, True, False)
                    with pe.Fori(0, EC // 4) as c:
                        pe.wait_ge(all_hot, w * (EC // 4) + c + 1)
                        for j in range(4):
                            ins = mm(one, hot_src[:, j, :], hot_key[:, j, :], False, False)
                        ins.then_inc(all_used, 1)
                    mm(one, zero16, iota_key, False, True).then_inc(all_summed, 1)
                    pe.wait_ge(all_stored, w + 1)
                for q in range(TPS - 1):
                    for t in range(ST):
                        sum_quarter(q, t, False)
                pe.wait_ge(w_back, 16)
                steps_of(False)
            with pe.Else():
                turn_rows(0)
                turn_weights()
                for what, n in first_plan():
                    if what == "W":
                        sum_window(0, n)
                    elif what == "R":
                        pe.wait_ge(slots_ready, 1)
                        turn_rows(1)
                    else:
                        sum_quarter(*n, True)
                steps_of(True)

            pe.wait_ge(zmax_ready, 1)
            spread_scale(1)

            def sum_out(q, where, col, nodes, b, free=True):
                if free:
                    pe.wait_ge(bank_read, q - 3)
                for t in range(ST):
                    ins = mm(b[0:nodes, :], where[:, t, col:col + nodes], parts[:, t, :], t == 0, t == ST - 1)
                ins.then_inc(out_summed, 1)

            pe.wait_ge(scale_ready, 2)
            for t in range(ST):
                if t % XC == 0:
                    pe.wait_ge(low_ready, NSPLIT + t // XC + 1)
                for n in range(TPS):
                    ins = mm(bank[n], strip(2)[:, t, n * P:(n + 1) * P], parts[:, t, :], t == 0, t == ST - 1)
                    if t == ST - 1:
                        ins.then_inc(out_summed, 1)
            for n in range(TPS):
                sum_out(TPS + n, strip(3), n * P, P, bank[TPS + n], False)
            with pe.Fori(2, NFULL - 2) as g:
                for n in range(TPS):
                    sum_out(g * TPS + n, strip(g + 2), n * P, P, bank[n])
            for q in range(LOOPED, ST):
                s, n, nodes = tile_of(q)
                if q == LOOPED + 1:
                    pe.wait_ge(early_back, 16)
                sum_out(q, last_strip if s == NFULL else strip(s), n * P, nodes, bank[TPS + q % TPS])


_INS = ["x", "src", "dst", "L0_gnn_W1l", "L0_gnn_b1l", "L0_gnn_W1r", "L0_gnn_W2l", "L0_gnn_b2l", "L0_gnn_W2r"]


def kernel(**inputs):
    import numpy as _np
    import concourse.bacc as _bacc
    from concourse import mybir as _mybir
    from concourse.bass_utils import run_bass_kernel_spmd as _run

    nc = _bacc.Bacc("TRN2", target_bir_lowering=False, num_devices=1)
    arrays, args = {}, []
    for name in _INS:
        a = _np.ascontiguousarray(inputs[name])
        arrays[f"in_{name}"] = a
        args.append(nc.dram_tensor(f"in_{name}", a.shape, _mybir.dt.from_np(a.dtype), kind="ExternalInput").ap())
    shape = inputs["x"].shape
    args.append(nc.dram_tensor("out_dram", shape, _mybir.dt.float32, kind="ExternalOutput").ap())
    bass_sage_resnorm(nc, *args)
    r = _run(nc, [arrays], core_ids=[0])
    return r.results[0]["out_dram"]
```

```python
import concourse.bass as bass
from concourse import mybir
from contextlib import ExitStack



def bass_sage_resnorm(nc: bass.Bass, x: bass.AP, src: bass.AP, dst: bass.AP, w1l: bass.AP, b1l: bass.AP,
                      w1r: bass.AP, w2l: bass.AP, b2l: bass.AP, w2r: bass.AP, out: bass.AP):
    fp32, fp16 = mybir.dt.float32, mybir.dt.float16
    i32, u32 = mybir.dt.int32, mybir.dt.uint32
    ALU = mybir.AluOpType
    ACT = mybir.ActivationFunctionType
    AX = mybir.AxisListType

    P = 128
    N, D = x.shape
    H = w1l.shape[0]
    E = src.shape[0]
    FT, HT = D // P, H // P
    ST = -(-N // P)
    NLAST = N - (ST - 1) * P
    PANE, PPW = 8, 2
    WIN = PPW * PANE
    NWIN = -(-N // WIN)
    NPANE = NWIN * PPW
    KEYS = ST * PANE
    TSTEP = 32
    STEP = PANE * TSTEP
    COLS = KEYS + PANE
    ROW = 32
    RPC = P // ROW
    CH = 2
    CPW = CH * PPW
    CAP = CH * RPC
    TR = -(-E // (P * ROW))
    EC = TR * ROW
    NROWS = P * TR
    EFULL = E // EC
    ETAIL = E - EFULL * EC
    FAR = 1 << 15
    SB = 512
    WPS, TPS = SB // WIN, SB // P
    NFULL = N // SB
    WLAST = NWIN - NFULL * WPS
    LASTW = WLAST * WIN
    GS = WPS * CPW
    NG = NFULL + 1
    XC = 5
    EPS = 1e-5
    EXP_SUM = float((127 + 14 + 127) << 23)
    EXP_MASK = 0x7F800000
    TINY = 2.0 ** -100
    assert KEYS <= STEP and NLAST <= LASTW <= P and ST == NFULL * TPS + 1 and WPS % 2 == 0 and WLAST % 2 == 0
    assert ST <= TSTEP and PPW * COLS <= SB and GS <= P and ST % XC == 0 and NPANE * PANE <= 8 * 2048
    assert NROWS + CAP <= 2048

    rows_dram = nc.dram_tensor("edge_rows", [NROWS + P, 2 * ROW], fp32, kind="Internal").ap()
    wT_dram = nc.dram_tensor("weights_transposed", [P, 2 * FT * H + HT * 2 * D], fp32, kind="Internal").ap()
    early_dram = nc.dram_tensor("counts_strips01", [2, P, ST * SB], fp16, kind="Internal").ap()
    zr_dram = nc.dram_tensor("z_and_residual", [ST * P, 2 * D], fp32, kind="Internal").ap()

    ctx = ExitStack()
    with ctx:
        def sb(name, shape, dt):
            return ctx.enter_context(nc.sbuf_tensor(name, shape, dt))[:]

        def sem(name):
            return ctx.enter_context(nc.semaphore(name))

        def carve(words):
            at = [0]

            def take(n, dt=fp32):
                a, at[0] = at[0], at[0] + n
                assert at[0] <= words.shape[1], (at[0], words.shape)
                return words[:, a:at[0]] if dt is fp32 else words[:, a:at[0]].bitcast(dt)
            return take

        counts = sb("counts", [P, NFULL * ST * SB + ST * LASTW], fp16)
        parts = sb("parts", [P, ST, 2 * D], fp16)
        WW = 2 * FT * H + HT * 2 * D
        work = sb("work", [P, WW], fp32)
        xs = sb("xs", [P, TPS, D], fp32)
        b2_row = sb("b2_row", [P, D], fp32)
        ident = sb("ident", [P, P], fp32)
        ones = sb("ones", [P, P], fp32)
        ones16 = sb("ones16", [P, P], fp16)
        b1T = sb("b1T", [P, HT], fp32)
        degree = sb("degree", [P, ST], fp32)
        column_sums = sb("column_sums", [P, SB], fp32)
        rdegree = sb("rdegree", [P, ST], fp32)
        zmax = sb("zmax", [P, ST], fp32)
        amax = sb("amax", [P, 2], fp32)
        scale = sb("scale", [P, 4], fp32)
        srow = sb("srow", [1, 8], fp32)
        half_max = sb("half_max", [P, 2], fp32)
        odd = sb("odd", [P, 1], fp32)
        frow = sb("frow", [1, 4], fp32)
        flag = sb("flag", [1, 1], i32)
        eps = sb("eps", [P, 1], fp32)
        warm = sb("warm", [P, 1], fp32)
        stats = sb("stats", [P, TPS, 6], fp32)
        moments = sb("moments", [P, TPS, 2], fp32)
        deviation = sb("deviation", [P, TPS, 3], fp32)

        take = carve(work)
        iota_key = take(KEYS // 2, fp16)
        iota_src = take(P * CPW // 2, fp16).rearrange("p (c r) -> p c r", r=CPW)
        iota_dst = take(CPW * PANE // 2, fp16).rearrange("p (r c) -> p r c", c=PANE)
        hot_key = take(2 * CPW * COLS // 2, fp16).rearrange("p (r c) -> p r c", c=COLS)
        hot_src = take(2 * CPW * P // 2, fp16).rearrange("p (b c r) -> p b c r", b=2, r=CPW)
        key_base = take(GS)
        group_base = take(NG)
        row_index = take(NG * RPC, u32)
        slot_key, slot_src, slot_dst = take(GS), take(GS // 2, fp16), take(GS // 2, fp16)
        gathers = take(2 * EC)
        rows = gathers[:, 0:2 * P].rearrange("p (i k e) -> p i k e", k=2, e=ROW)
        unmixed = gathers[:, 2 * P:4 * P].rearrange("p (k e) -> p k e", k=2)
        slot_whole = gathers[:, 4 * P:4 * P + GS].bitcast(i32)
        all_keys, all_srcs = gathers[:, 0:EC], gathers[:, EC:2 * EC]
        first_degrees = take(SB), take(SB)
        zero16 = first_degrees[0][:, 0:P // 2].bitcast(fp16)
        take = carve(work)
        z_in = [take(XC * D).rearrange("p (t f) -> p t f", f=D) for _ in range(2)]
        y = take(TPS * D).rearrange("p (n f) -> p n f", f=D)

        def split_weights(words):
            return (words[:, 0:2 * FT * H].rearrange("p (k h) -> p k h", h=H),
                    words[:, 2 * FT * H:].rearrange("p (m o) -> p m o", o=2 * D))

        STRIP = ST * SB // 2
        weights_first = counts[:, 2 * STRIP * (NFULL - 1):2 * STRIP * (NFULL - 1) + 2 * WW].bitcast(fp32)
        weights_later = counts[:, 2 * STRIP:2 * STRIP + 2 * WW].bitcast(fp32)

        take = carve(counts[:, 2 * STRIP * 2:2 * STRIP * (NFULL - 1)].bitcast(fp32))
        x_in = take(ST * D).rearrange("p (t f) -> p t f", f=D)
        w1_in = take(2 * HT * D).rearrange("p (k m f) -> p k m f", k=2, f=D)
        w2_in = take(2 * FT * H).rearrange("p (k o h) -> p k o h", k=2, h=H)
        keys = take(2 * EC).rearrange("p (r k e) -> p r k e", k=2, e=ROW)
        pad_rows = take(2 * ROW)
        dst_i, dst_next, src_i = take(EC, i32), take(EC, i32), take(EC, i32)
        k_win, k_dst, k_tile, k_src, k_sum = (take(EC, i32) for _ in range(5))
        disorder = take(EC)
        first_dst = take(TR)
        pane_start = take((NPANE + 2) // 2, fp16)[:, 0:NPANE + 1]
        take = carve(counts[:, 2 * STRIP:2 * STRIP * 2].bitcast(fp32))
        starts_below = take(TR * ((NPANE + 2) // 2), fp16).rearrange("p (t w) -> p t w", t=TR)[:, :, 0:NPANE + 1]
        rows_below = take(NPANE + 1)
        first_row = take(NPANE)
        row_span = take(NPANE)
        slot_row = take(NG * GS // 2, fp16)
        slot_in = take(NG * GS // 2, fp16)
        quarter = take(NG * RPC)

        take = carve(counts[:, 0:ST * SB].bitcast(fp32))
        hT = take(HT * SB).rearrange("p (m c) -> p m c", c=SB)
        aggT = take(FT * SB).rearrange("p (k c) -> p k c", c=SB)
        xT = take(FT * SB).rearrange("p (k c) -> p k c", c=SB)
        later_degrees = take(SB), take(SB)
        z_out = take(2 * D).rearrange("p (b f) -> p b f", b=2)

        bank = [ctx.enter_context(nc.psum_tensor(f"bank{i}", [P, 512], fp32))[:] for i in range(8)]

        def strip(s):
            return counts[:, bass.ds(s * (ST * SB), ST * SB)].rearrange("p (t c) -> p t c", c=SB)

        last_strip = counts[:, NFULL * ST * SB:].rearrange("p (t c) -> p t c", c=LASTW)

        def windows(bank_):
            panes = bank_[:, 0:PPW * COLS].rearrange("p (u x) -> p u x", x=COLS)
            return panes[:, :, 0:KEYS].rearrange("p u (t c) -> p t u c", c=PANE)

        def window_columns(bank_):
            return bank_[:, 0:PPW * COLS].rearrange("p (u x) -> p u x", x=COLS)[:, :, KEYS:COLS]

        edges_in = sem("edges_in")
        next_in = sem("next_in")
        x_loaded = [sem(f"x_loaded{i}") for i in range(2)]
        w_in = sem("w_in")
        bias_in = sem("bias_in")
        b2_in = sem("b2_in")
        padded = sem("padded")
        consts = sem("consts")
        idents = sem("idents")
        prep = sem("prep")
        below_ready = sem("below_ready")
        rows_counted = sem("rows_counted")
        order_ready = sem("order_ready")
        order_summed = sem("order_summed")
        flag_ready = sem("flag_ready")
        eps_ready = sem("eps_ready")
        keys_ready = sem("keys_ready")
        rows_stored = sem("rows_stored")
        slot_row_ready = sem("slot_row_ready")
        slot_row_turned = sem("slot_row_turned")
        index_ready = sem("index_ready")
        xmax_ready = sem("xmax_ready")
        max_turned = sem("max_turned")
        scale_row = sem("scale_row")
        scale_spread = sem("scale_spread")
        scale_ready = sem("scale_ready")
        unscale_ready = sem("unscale_ready")
        high_ready = sem("high_ready")
        x_scaled = sem("x_scaled")
        low_ready = sem("low_ready")
        w_turned = sem("w_turned")
        w_copied = sem("w_copied")
        w_stored = sem("w_stored")
        w_back = sem("w_back")
        gathered = sem("gathered")
        rows_unmixed = sem("rows_unmixed")
        rows_turned = sem("rows_turned")
        slots_ready = sem("slots_ready")
        slots_whole = sem("slots_whole")
        slots_shifted = sem("slots_shifted")
        slots_dst = sem("slots_dst")
        columns_summed = sem("columns_summed")
        hot_ready = sem("hot_ready")
        window_summed = sem("window_summed")
        window_stored = sem("window_stored")
        early_out = [sem(f"early_out{i}") for i in range(2)]
        early_back = sem("early_back")
        all_in = sem("all_in")
        all_keyed = sem("all_keyed")
        all_hot = sem("all_hot")
        all_used = sem("all_used")
        all_summed = sem("all_summed")
        all_stored = sem("all_stored")
        xs_in = sem("xs_in")
        last_x_in = sem("last_x_in")
        turned = sem("turned")
        turned_copied = sem("turned_copied")
        degree_summed = sem("degree_summed")
        agg_summed = sem("agg_summed")
        degree_ready = sem("degree_ready")
        inverse_ready = sem("inverse_ready")
        agg_ready = sem("agg_ready")
        h_summed = sem("h_summed")
        h_ready = sem("h_ready")
        zr_summed = sem("zr_summed")
        z_copied = sem("z_copied")
        r_added = sem("r_added")
        b2_added = sem("b2_added")
        z_stored = [sem(f"z_stored{b}") for b in range(2)]
        r_stored = sem("r_stored")
        z_loaded = [sem(f"z_loaded{b}") for b in range(2)]
        zmax_ready = sem("zmax_ready")
        rdegree_ready = sem("rdegree_ready")
        out_summed = sem("out_summed")
        res_in = [sem(f"res_in{n}") for n in range(TPS)]
        high_joined = sem("high_joined")
        bank_read = sem("bank_read")
        stats_ready = sem("stats_ready")
        moments_ready = sem("moments_ready")
        root_ready = sem("root_ready")
        root_inverted = sem("root_inverted")
        factors_ready = sem("factors_ready")
        normed = sem("normed")
        out_stored = [sem(f"out_stored{n}") for n in range(TPS)]

        NSPLIT = ST // XC
        HALF = ST // 2
        LEAD = 3.0
        WBANKS = 2 * FT + HT
        MAIN = E - ETAIL
        TURNS = FT + 1
        QUARTER = SB // TPS
        WPQ = WPS // TPS
        AGG, ZR, HID, WEIGHTS, TURN = (0, 1), (0, 1), (3, 4), (3, 4), 5
        DEG, BUILT = 2, (6, 7)

        def layer_plan(s, built):
            if s == 0:
                pieces = [("D", 0, 0.85), ("E", 0, 0.0)]
                for t in range(ST):
                    pieces.append(("Q", (TPS - 1, t), 0.22))
                    if t % XC == XC - 1 and t < ST - 1:
                        pieces.append(("I", t // XC, 0.0))
                pieces.append(("F", 0, 0.0))
                pieces += [("X", 0, 0.6), ("X", 1, 0.6), ("G", 0, 0.2)]
            else:
                pieces = [("D", 0, 0.85), ("E", 0, 0.0)]
                for t in range(ST):
                    pieces.append(("A", t, 0.86))
                    if t % 3 == 2 and t // 3 < (TPS if s < NFULL else 1):
                        pieces.append(("I", t // 3, 0.0))
                    if t in (12, 15):
                        pieces.append(("X", (t - 12) // 3, 0.6))
                    if t == 18:
                        pieces.append(("G", 0, 0.2))
                pieces.append(("F", 0, 0.0))
            pieces += [("H", (m, half), 1.75) for m in range(HT) for half in range(2)]
            pieces += [("Z", (n, half), 1.75) for n in range(TPS if s < NFULL else 1) for half in range(2)]
            total = sum(time for _, _, time in pieces[:-1])
            lead = 0.0 if s == 0 else LEAD
            free = built if built == WPS else 0
            plan, windows_, spent = [], 0, 0.0
            for what, n, time in pieces:
                plan.append((what, n))
                if what == "A" and n % XC == 3 and windows_ < built < WPS:
                    plan.append(("W", windows_))
                    windows_ += 1
                spent += time
                while windows_ < min(free * (spent - lead) / (total - lead) - 1e-9, built):
                    plan.append(("W", windows_))
                    windows_ += 1
            if built == WPS and s + 2 < NG:
                plan.append(("R", 0))
            while windows_ < built:
                plan.append(("W", windows_))
                windows_ += 1
            return plan

        def first_plan():
            plan = [("U", 0)]
            for k in range(WPQ):
                plan.append(("W", k))
                if k == 1:
                    plan.append(("P", 0))
                if k % 2:
                    plan.append(("S", k // 2))
                elif k >= 2:
                    plan.append(("T", k // 2 - 1))
                if k == WPQ - 2:
                    plan.append(("U", 1))
            turned_ = WPQ // 2 - 1
            for q in range(TPS - 1):
                done = 0
                for k in range(WPQ):
                    plan.append(("W", (q + 1) * WPQ + k))
                    if q == 0 and k == 0:
                        plan.append(("S", NSPLIT - 1))
                    if turned_ < WBANKS:
                        plan.append(("T", turned_))
                        turned_ += 1
                    if q == TPS - 2 and k == WPQ - 3:
                        plan.append(("R", 0))
                    until = ST * (k + 1) // WPQ
                    plan += [("Q", (q, t)) for t in range(done, until)]
                    done = until
            return plan

        def windows_in(s):
            return 0 if s > NFULL else WLAST if s == NFULL else WPS

        def run_layers(engine, step, build):
            for s in (0, 1):
                step(s, layer_plan(s, windows_in(s + 1) if build else 0), s)
            with engine.Fori(2, NFULL - 1) as s:
                step(s, layer_plan(2, WPS if build else 0), 2)
            step(NFULL - 1, layer_plan(NFULL - 1, WLAST if build else 0), NFULL - 1)
            step(NFULL, layer_plan(NFULL, 0), NFULL)

        def tiles_of(kind):
            return (1, NLAST, NLAST) if kind == NFULL else (TPS, P, SB)

        def xs_of(kind):
            return y if kind == NFULL else xs

        def degrees_of(kind, build):
            return first_degrees if kind == 0 and build else later_degrees

        def full_rows(ap, first=0):
            return ap[first:first + MAIN].rearrange("(p e) -> p e", e=EC)

        def tail_row(ap, first, n):
            return ap[first:first + n].rearrange("(p e) -> p e", p=1)

        LOOPED = (NFULL - 2) * TPS

        def tile_of(q):
            if q < LOOPED:
                return 2 + q // TPS, q % TPS, P
            if q == LOOPED:
                return NFULL, 0, NLAST
            return (q - LOOPED - 1) // TPS, (q - LOOPED - 1) % TPS, P

        block = ctx.enter_context(nc.Block())

        @block.sync
        def _(sp):
            sp.wait_ge(padded, 3)
            sp.dma_start(dst_i[0:EFULL, :], full_rows(dst)).then_inc(edges_in, 16)
            sp.dma_start(dst_i[EFULL:EFULL + 1, 0:ETAIL], tail_row(dst, MAIN, ETAIL)).then_inc(edges_in, 16)
            sp.dma_start(src_i[0:EFULL, :], full_rows(src)).then_inc(edges_in, 16)
            sp.dma_start(src_i[EFULL:EFULL + 1, 0:ETAIL], tail_row(src, MAIN, ETAIL)).then_inc(edges_in, 16)
            sp.dma_start(dst_next[0:EFULL, :], full_rows(dst, 1)).then_inc(next_in, 16)
            sp.dma_start(dst_next[EFULL:EFULL + 1, 0:ETAIL - 1],
                         tail_row(dst, MAIN + 1, ETAIL - 1)).then_inc(next_in, 16)
            sp.dma_start(x_in[:, 0:HALF, :],
                         x[0:HALF * P, :].rearrange("(t p) f -> p t f", p=P)).then_inc(x_loaded[0], 16)
            sp.wait_ge(keys_ready, 2)
            sp.dma_start(rows_dram[0:NROWS, :].rearrange("(p r) c -> p (r c)", r=TR),
                         keys.rearrange("p r k e -> p (r k e)")).then_inc(rows_stored, 16)
            sp.dma_start(rows_dram[NROWS:NROWS + P, :], pad_rows).then_inc(rows_stored, 16)
            sp.wait_ge(padded, 4)
            sp.dma_start(x_in[:, HALF:ST - 1, :],
                         x[HALF * P:(ST - 1) * P, :].rearrange("(t p) f -> p t f", p=P)).then_inc(x_loaded[1], 16)
            sp.dma_start(x_in[0:NLAST, ST - 1, :], x[(ST - 1) * P:N, :]).then_inc(x_loaded[1], 16)
            sp.dma_start(b2_row, b2l.partition_broadcast(P)).then_inc(b2_in, 16)
            sp.wait_ge(w_copied, WBANKS)
            sp.dma_start(wT_dram, weights_first).then_inc(w_stored, 16)

            def spill(s):
                sp.dma_start(early_dram[s], counts[:, 2 * STRIP * s:2 * STRIP * (s + 1)]).then_inc(early_out[s], 16)

            def load_xs(s, kind):
                tiles, nodes, _ = tiles_of(kind)
                sp.dma_start(xs_of(kind)[0:nodes, 0:tiles, :],
                             x[bass.ds(s * SB, nodes * tiles), :].rearrange("(n p) f -> p n f", p=nodes))\
                    .then_inc(last_x_in if kind == NFULL else xs_in, 16)

            load_xs(0, 0)

            def steps(build):
                def step(s, plan, kind):
                    tiles, nodes, _ = tiles_of(kind)
                    if kind == 1 and build:
                        sp.wait_ge(window_stored, 2 * WPS)
                        spill(1)
                    if 0 < kind < NFULL:
                        sp.wait_ge(r_stored, s * 16)
                        load_xs(s, kind)
                    if kind == NFULL - 1:
                        if build:
                            sp.wait_ge(window_stored, NWIN)
                        load_xs(NFULL, NFULL)
                    if kind == 1:
                        sp.wait_ge(early_out[1], 16)
                        sp.wait_ge(agg_summed, 2)
                        sp.wait_ge(w_stored, 16)
                        sp.dma_start(weights_later, wT_dram).then_inc(w_back, 16)
                    if kind == NFULL:
                        prefetch_z()
                    for n in range(tiles):
                        sp.wait_ge(z_copied, s * TPS + n + 1)
                        sp.dma_start(zr_dram[bass.ds(s * SB + n * P, nodes), 0:D], z_out[0:nodes, n % 2, :])\
                            .then_inc(z_stored[n % 2], 16)
                    sp.wait_ge(r_added, s * TPS + tiles)
                    sp.dma_start(zr_dram[bass.ds(s * SB, nodes * tiles), D:2 * D]
                                 .rearrange("(n p) f -> p n f", p=nodes), xs_of(kind)[0:nodes, 0:tiles, :])\
                        .then_inc(r_stored, 16)
                run_layers(sp, step, build)

            def load_z(c):
                full = XC if c < NSPLIT - 1 else XC - 1
                sp.dma_start(z_in[c % 2][:, 0:full, :],
                             zr_dram[c * XC * P:(c * XC + full) * P, 0:D].rearrange("(t p) f -> p t f", p=P))\
                    .then_inc(z_loaded[c % 2], 16)
                if full < XC:
                    sp.dma_start(z_in[c % 2][0:NLAST, full, :], zr_dram[(ST - 1) * P:N, 0:D])\
                        .then_inc(z_loaded[c % 2], 16)

            def prefetch_z():
                for b in range(2):
                    sp.wait_ge(z_stored[b], 16 * NFULL * TPS // 2)
                load_z(0)
                load_z(1)

            sp.wait_ge(flag_ready, 1)
            slow = sp.value_load(flag[0:1, 0:1])
            with sp.If(slow > 0):
                sp.wait_ge(rows_stored, 32)
                sp.wait_ge(gathered, RPC * 16)
                back = rows_dram[0:NROWS, :].rearrange("(p r) (k e) -> p r k e", r=TR, k=2)
                sp.dma_start(all_keys.rearrange("p (r e) -> p r e", e=ROW), back[:, :, 0, :]).then_inc(all_in, 16)
                sp.dma_start(all_srcs.rearrange("p (r e) -> p r e", e=ROW), back[:, :, 1, :]).then_inc(all_in, 16)
                sp.wait_ge(w_stored, 16)
                sp.wait_ge(all_stored, NPANE)
                sp.wait_ge(all_keyed, NPANE)
                sp.dma_start(work, wT_dram).then_inc(w_back, 16)
                spill(0)
                spill(1)
                steps(False)
            with sp.Else():
                sp.wait_ge(window_stored, WPS)
                spill(0)
                steps(True)

            sp.wait_ge(z_stored[0], 16 * (NFULL * TPS // 2 + 1))
            for c in range(2, NSPLIT):
                sp.wait_ge(low_ready, NSPLIT + c)
                load_z(c)
            sp.wait_ge(zr_summed, NFULL * TPS + 1)
            sp.dma_start(counts[:, 0:4 * STRIP].rearrange("p (s c) -> p s c", s=2),
                         early_dram.rearrange("s p c -> p s c")).then_inc(early_back, 16)

            def load_res(t, n, nodes):
                sp.dma_start(y[0:nodes, n, :], zr_dram[bass.ds(t * P, nodes), D:2 * D]).then_inc(res_in[n], 16)

            def store_out(q, t, n, nodes):
                sp.wait_ge(normed, q + 1)
                sp.dma_start(out[bass.ds(t * P, nodes), :], y[0:nodes, n, :]).then_inc(out_stored[n], 16)

            sp.wait_ge(r_stored, 16 * NG)
            for n in range(TPS):
                load_res(2 * TPS + n, n, P)
            with sp.Fori(1, NFULL - 2) as g:
                for n in range(TPS):
                    store_out((g - 1) * TPS + n, (g + 1) * TPS + n, n, P)
                    sp.wait_ge(out_stored[n], g * 16)
                    load_res((g + 2) * TPS + n, n, P)
            for q in range(LOOPED - TPS, ST):
                s, n, nodes = tile_of(q)
                store_out(q, s * TPS + n, q % TPS, nodes)
                if q + TPS < ST:
                    s, n, nodes = tile_of(q + TPS)
                    sp.wait_ge(out_stored[q % TPS], 16 * (q // TPS + 1))
                    load_res(s * TPS + n, q % TPS, nodes)
            for n in range(TPS):
                sp.wait_ge(out_stored[n], 16 * len(range(n, ST, TPS)))

        @block.gpsimd
        def _(pool):
            G = nc.gpsimd
            G.memset(dst_i, FAR).then_inc(padded, 1)
            G.memset(dst_next, FAR).then_inc(padded, 1)
            G.memset(src_i, 0).then_inc(padded, 1)
            G.memset(x_in[:, ST - 1, :], 0.0).then_inc(padded, 1)

            def ramp(where, pattern):
                G.iota(where, pattern, base=0, channel_multiplier=0,
                       allow_small_or_imprecise_dtypes=True).then_inc(consts, 1)

            ramp(pane_start, [[PANE, NPANE + 1]])
            G.memset(ones16, 1.0).then_inc(consts, 1)
            G.memset(ones, 1.0).then_inc(consts, 1)
            G.memset(ident, 0.0).then_inc(idents, 1)
            pool.wait_ge(idents, 1)
            G.affine_select(out=ident, in_=ident, compare_op=ALU.not_equal, fill=1.0, base=0,
                            pattern=[[-1, P]], channel_multiplier=1).then_inc(consts, 1)
            ramp(slot_in[0:1, :], [[0, NG * WPS * PPW], [RPC, CH]])
            ramp(quarter, [[0, NG], [1, RPC]])
            ramp(key_base, [[STEP, WPS * PPW], [0, CH]])
            ramp(group_base, [[-STEP * WPS * PPW, NG]])
            ramp(iota_key, [[1, ST], [TSTEP, PANE]])
            ramp(iota_dst, [[0, CPW], [1, PANE]])
            ramp(iota_src, [[1, P], [0, CPW]])
            G.memset(zero16, 0.0).then_inc(consts, 1)

            def low_parts():
                for c in range(NSPLIT):
                    value, tiles = x_in[:, c * XC:(c + 1) * XC, :], slice(c * XC, (c + 1) * XC)
                    pool.wait_ge(high_ready, c + 1)
                    G.tensor_tensor(parts[:, tiles, D:2 * D], value, parts[:, tiles, 0:D], ALU.subtract)\
                        .then_inc(low_ready, 1)

            def gather(g):
                if g >= 1:
                    pool.wait_ge(rows_unmixed, g)
                for i in range(RPC):
                    G.indirect_dma_start(
                        rows[0:GS, i].rearrange("p k e -> p (k e)"), None, rows_dram,
                        bass.IndirectOffsetOnAxis(row_index[0:GS, g * RPC + i:g * RPC + i + 1], 0))\
                        .then_inc(gathered, 16)

            def add_b2(s):
                tiles, nodes, _ = tiles_of(s)
                pool.wait_ge(turned, s * TURNS + FT)
                b2 = b2_row[0:nodes, :].rearrange("p (o f) -> p o f", o=1).broadcast_to([nodes, tiles, D])
                here = xs_of(s)[0:nodes, 0:tiles, :]
                G.tensor_tensor(here, here, b2, ALU.add).then_inc(b2_added, 1)

            pool.wait_ge(rows_stored, 32)
            pool.wait_ge(index_ready, 1)
            gather(0)
            pool.wait_ge(flag_ready, 1)
            pool.wait_ge(b2_in, 16)
            slow = pool.value_load(flag[0:1, 0:1])
            with pool.If(slow > 0):
                low_parts()
                for s in range(NG):
                    add_b2(s)
            with pool.Else():
                gather(1)
                low_parts()
                gather(2)
                for s in range(NG):
                    if s + 3 < NG:
                        gather(s + 3)
                    add_b2(s)

        @block.vector
        def _(dve):
            V = nc.vector
            steps = [0]

            def then(ins):
                ins.then_inc(prep, 1)
                steps[0] += 1
                dve.wait_ge(prep, steps[0])

            def find_scale(which):
                dve.wait_ge(max_turned, which + 1)
                then(V.tensor_reduce(srow[0:1, 0:1], bank[DEG][0:1, 0:P], AX.X, ALU.max))
                then(V.tensor_scalar(srow[0:1, 1:2], srow[0:1, 0:1], TINY, None, ALU.max))
                then(V.tensor_scalar(srow[0:1, 2:3].bitcast(i32), srow[0:1, 1:2].bitcast(i32), EXP_MASK, None,
                                     ALU.bitwise_and))
                V.tensor_scalar(srow[0:1, 3:4].bitcast(i32), srow[0:1, 2:3].bitcast(i32), -1.0, EXP_SUM,
                                ALU.mult, ALU.add).then_inc(scale_row, 1)
                dve.wait_ge(scale_spread, which + 1)
                V.tensor_copy(scale[:, which:which + 1], bank[DEG][:, 256:257]).then_inc(scale_ready, 1)
                dve.wait_ge(scale_ready, which + 1)
                V.reciprocal(scale[:, 2 + which:3 + which], scale[:, which:which + 1]).then_inc(unscale_ready, 1)

            V.memset(eps, EPS).then_inc(eps_ready, 1)
            V.memset(zmax, 0.0)
            V.memset(degree, 1.0)
            V.memset(slot_row[0:1, NPANE * CH:], 0.0)
            V.memset(pad_rows, -1.0).then_inc(keys_ready, 1)
            dve.wait_ge(edges_in, 4 * 16)
            then(V.tensor_copy(first_dst, dst_i[:, 0:EC:ROW]))
            dve.wait_ge(consts, 1)
            for t in range(TR):
                V.tensor_scalar(starts_below[:, t, :], pane_start, first_dst[:, t:t + 1], None, ALU.is_gt)\
                    .then_inc(below_ready, 1)
            V.tensor_scalar(k_win, dst_i, PANE.bit_length() - 1, STEP.bit_length() - 1,
                            ALU.arith_shift_right, ALU.logical_shift_left)
            V.tensor_scalar(k_dst, dst_i, PANE - 1, TSTEP.bit_length() - 1, ALU.bitwise_and, ALU.logical_shift_left)
            V.tensor_scalar(k_tile, src_i, P.bit_length() - 1, None, ALU.arith_shift_right)
            then(V.tensor_scalar(k_src, src_i, P - 1, None, ALU.bitwise_and))
            then(V.tensor_tensor(k_sum, k_win, k_dst, ALU.add))
            V.tensor_tensor(keys[:, :, 0, :], k_sum.rearrange("p (r e) -> p r e", e=ROW),
                            k_tile.rearrange("p (r e) -> p r e", e=ROW), ALU.add)
            V.tensor_copy(keys[:, :, 1, :], k_src.rearrange("p (r e) -> p r e", e=ROW)).then_inc(keys_ready, 1)
            dve.wait_ge(rows_counted, 1)
            then(V.tensor_copy(rows_below[0:1, :], bank[DEG][0:1, 0:NPANE + 1]))
            then(V.tensor_scalar(first_row[0:1, :], rows_below[0:1, 0:NPANE], -1.0, 0.0, ALU.add, ALU.max))
            dve.wait_ge(consts, 6)
            first3 = first_row[0:1, :].rearrange("p (w o) -> p w o", o=1).broadcast_to([1, NPANE, CH])
            V.tensor_tensor(slot_row[0:1, 0:NPANE * CH].rearrange("p (w c) -> p w c", c=CH), first3,
                            slot_in[0:1, 0:NPANE * CH].rearrange("p (w c) -> p w c", c=CH), ALU.add)\
                .then_inc(slot_row_ready, 1)
            dve.wait_ge(next_in, 32)
            then(V.tensor_tensor(disorder, dst_i, dst_next, ALU.is_gt))
            V.tensor_reduce(odd, disorder, AX.X, ALU.add).then_inc(order_ready, 1)
            dve.wait_ge(slot_row_turned, 1)
            V.tensor_tensor(row_index[0:GS, :], bank[DEG][0:GS, 320:320 + NG * RPC], quarter[0:GS, :],
                            ALU.add).then_inc(index_ready, 1)
            then(V.tensor_tensor(row_span[0:1, :], rows_below[0:1, 1:], first_row[0:1, :], ALU.subtract))
            then(V.tensor_reduce(frow[0:1, 0:1], row_span[0:1, :], AX.X, ALU.max))
            then(V.tensor_scalar(frow[0:1, 1:2], frow[0:1, 0:1], float(CAP), None, ALU.is_gt))
            dve.wait_ge(order_summed, 1)
            V.tensor_tensor(flag, frow[0:1, 1:2], bank[DEG][0:1, 256:257], ALU.add).then_inc(flag_ready, 1)

            for i, (first, last) in enumerate([(0, HALF), (HALF, ST)]):
                dve.wait_ge(x_loaded[i], 16 * (i + 1))
                ins = V.tensor_reduce(half_max[:, i:i + 1], x_in[:, first:last, :].rearrange("p t f -> p (t f)"),
                                      AX.X, ALU.max, apply_absolute_value=True)
            then(ins)
            V.tensor_reduce(amax[:, 0:1], half_max, AX.X, ALU.max).then_inc(xmax_ready, 1)

            def scale_x(c):
                value = x_in[:, c * XC:(c + 1) * XC, :]
                V.tensor_scalar(value, value, scale[:, 0:1], None, ALU.mult).then_inc(x_scaled, 1)

            def take_slots(g, first=False):
                if not first:
                    dve.wait_ge(hot_ready, g * GS)
                dve.wait_ge(rows_turned, g + 1)
                V.scalar_tensor_tensor(out=slot_key, in0=bank[TURN][:, 0:GS], scalar=group_base[:, bass.ds(g, 1)],
                                       in1=key_base, op0=ALU.add, op1=ALU.subtract)
                V.tensor_copy(slot_src, bank[TURN][:, P:P + GS]).then_inc(slots_ready, 1)
                dve.wait_ge(slots_ready, g + 1)
                V.tensor_copy(slot_whole, slot_key).then_inc(slots_whole, 1)
                dve.wait_ge(slots_whole, g + 1)
                V.tensor_scalar(slot_whole, slot_whole, TSTEP.bit_length() - 1, None, ALU.arith_shift_right)\
                    .then_inc(slots_shifted, 1)
                dve.wait_ge(slots_shifted, g + 1)
                V.tensor_copy(slot_dst, slot_whole).then_inc(slots_dst, 1)
                dve.wait_ge(slots_dst, g + 1)

            def window_hots(b, k, first=False):
                if not first:
                    dve.wait_ge(window_summed, b * WPS + (k - 1))
                src_ = slot_src[:, k * CPW:(k + 1) * CPW].rearrange("p (o r) -> p o r", o=1)
                V.tensor_tensor(hot_src[:, k % 2], iota_src, src_.broadcast_to([P, P, CPW]), ALU.is_equal)
                dst_ = slot_dst[:, k * CPW:(k + 1) * CPW].rearrange("p (r o) -> p r o", o=1)
                V.tensor_tensor(hot_key[:, (k % 2) * CPW:(k % 2 + 1) * CPW, KEYS:COLS], iota_dst,
                                dst_.broadcast_to([P, CPW, PANE]), ALU.is_equal)
                for j in range(CPW):
                    V.tensor_scalar(hot_key[:, (k % 2) * CPW + j, 0:KEYS], iota_key,
                                    slot_key[:, k * CPW + j:k * CPW + j + 1], None, ALU.is_equal)\
                        .then_inc(hot_ready, 1)

            def sum_columns(s, kind):
                where = last_strip if kind == NFULL else strip(s)
                if kind:
                    dve.wait_ge(degree_summed, s)
                V.tensor_reduce(column_sums[:, 0:where.shape[2]], where.rearrange("p t c -> p c t"), AX.X, ALU.add)\
                    .then_inc(columns_summed, 1)

            def take_degrees(s, kind, build):
                cols = tiles_of(kind)[2]
                max_degree, inv_degree = degrees_of(kind, build)
                dve.wait_ge(degree_summed, s + 1)
                if kind == 0 and not build:
                    dve.wait_ge(agg_summed, 1)
                    dve.wait_ge(early_out[0], 16)
                elif kind:
                    dve.wait_ge(turned, s * TURNS)
                V.tensor_scalar(max_degree[:, 0:cols], bank[DEG][:, 0:cols], 1.0, None, ALU.max)\
                    .then_inc(degree_ready, 1)

            def invert_degrees(s, kind, build, n):
                nodes = tiles_of(kind)[1]
                max_degree, inv_degree = degrees_of(kind, build)
                dve.wait_ge(degree_ready, s + 1)
                V.reciprocal(inv_degree[:, n * P:n * P + nodes], max_degree[:, n * P:n * P + nodes])\
                    .then_inc(inverse_ready, 1)

            def take_sums(s, kind, build):
                cols = tiles_of(kind)[2]
                inv_degree = degrees_of(kind, build)[1]
                dve.wait_ge(agg_summed, s + 1)
                dve.wait_ge(inverse_ready, s * TPS + tiles_of(kind)[0])
                if kind == 0:
                    dve.wait_ge(early_out[0], 16)
                if kind:
                    dve.wait_ge(h_summed, s * HT)
                dve.wait_ge(unscale_ready, 1)
                for k in range(FT):
                    V.scalar_tensor_tensor(out=aggT[:, k, 0:cols], in0=bank[AGG[k]][:, 0:cols], scalar=scale[:, 2:3],
                                           in1=inv_degree[:, 0:cols], op0=ALU.mult, op1=ALU.mult)\
                        .then_inc(agg_ready, 1)

            def take_outputs(s, kind, n):
                nodes = tiles_of(kind)[1]
                b = bank[ZR[n % 2]]
                if n == 0:
                    dve.wait_ge(b2_added, s + 1)
                dve.wait_ge(z_copied, s * TPS + n + 1)
                V.tensor_reduce(zmax[0:nodes, bass.ds(s * TPS + n, 1)], b[0:nodes, 0:D], AX.X, ALU.max,
                                apply_absolute_value=True)
                here = xs_of(kind)[0:nodes, n, :]
                V.tensor_tensor(here, b[0:nodes, D:2 * D], here, ALU.add)\
                    .then_inc(r_added, 1)

            def follow(s, plan, kind, b, build):
                windows_ = sum(what == "W" for what, _ in plan)
                if not build:
                    sum_columns(s, kind)
                made = passed = 0
                for what, n in plan:
                    if what == "W":
                        passed += 1
                    if what in "EIFZ":
                        while made < min(passed + 2, windows_):
                            window_hots(b, made)
                            made += 1
                        if what == "E":
                            if kind or build:
                                take_degrees(s, kind, build)
                        elif what == "I":
                            if kind or build:
                                invert_degrees(s, kind, build, n)
                        elif what == "F":
                            if kind == 0 and not build:
                                take_degrees(s, kind, build)
                                for tile in range(TPS):
                                    invert_degrees(s, kind, build, tile)
                            take_sums(s, kind, build)
                        else:
                            if n[1]:
                                take_outputs(s, kind, n[0])
                while made < windows_:
                    window_hots(b, made)
                    made += 1
                if any(what == "R" for what, _ in plan):
                    take_slots(s + 2)

            def steps_of(build):
                run_layers(dve, lambda s, plan, kind: follow(s, plan, kind, s + 1, build), build)

            dve.wait_ge(consts, 12)
            dve.wait_ge(flag_ready, 1)
            slow = dve.value_load(flag[0:1, 0:1])
            before = steps[0]
            with dve.If(slow > 0):
                find_scale(0)
                for c in range(NSPLIT):
                    scale_x(c)
                dve.wait_ge(all_in, 32)
                with dve.Fori(0, NPANE) as w:
                    with dve.Fori(0, EC // CPW) as c:
                        dve.wait_ge(all_used, w * (EC // CPW) + c + 1)
                        src_ = all_srcs[:, bass.ds(c * CPW, CPW)].rearrange("p (o r) -> p o r", o=1)
                        V.tensor_tensor(hot_src[:, 0], iota_src, src_.broadcast_to([P, P, CPW]), ALU.is_equal)
                        for j in range(CPW):
                            ins = V.tensor_scalar(hot_key[:, j, 0:KEYS], iota_key, all_keys[:, bass.ds(c * CPW + j, 1)],
                                                  None, ALU.is_equal)
                        ins.then_inc(all_hot, 1)
                    dve.wait_ge(all_hot, w * (EC // CPW) + EC // CPW)
                    V.tensor_scalar(all_keys, all_keys, float(-STEP), None, ALU.add).then_inc(all_keyed, 1)
                    dve.wait_ge(all_keyed, w + 1)
                steps_of(False)
            with dve.Else():
                steps[0] = before
                take_slots(0, True)
                for k in range(2):
                    window_hots(0, k, True)
                find_scale(0)
                for k in range(2, WPS):
                    if k % 2 == 0 and k // 2 <= NSPLIT:
                        scale_x(k // 2 - 1)
                    window_hots(0, k)
                take_slots(1)
                steps_of(True)

            def low_part(value, nodes, t0, n, which):
                return V.scalar_tensor_tensor(
                    out=parts[0:nodes, t0:t0 + n, D:2 * D], in0=value, scalar=scale[0:nodes, which:which + 1],
                    in1=parts[0:nodes, t0:t0 + n, 0:D], op0=ALU.mult, op1=ALU.subtract)

            dve.wait_ge(r_added, NFULL * TPS + 1)
            V.tensor_reduce(amax[:, 1:2], zmax, AX.X, ALU.max).then_inc(zmax_ready, 1)
            find_scale(1)
            dve.wait_ge(high_ready, NSPLIT + 1)
            low_part(z_in[0][:, 0:1, :], P, 0, 1, 1).then_inc(low_ready, 1)
            for c in range(NSPLIT):
                dve.wait_ge(high_ready, NSPLIT + c + 2)
                if c == 0:
                    low_part(z_in[0][:, 1:XC, :], P, 1, XC - 1, 1).then_inc(low_ready, 1)
                elif c < NSPLIT - 1:
                    low_part(z_in[c % 2], P, c * XC, XC, 1).then_inc(low_ready, 1)
                else:
                    low_part(z_in[c % 2][:, 0:XC - 1, :], P, c * XC, XC - 1, 1)
                    low_part(z_in[c % 2][0:NLAST, XC - 1:XC, :], NLAST, ST - 1, 1, 1).then_inc(low_ready, 1)
            dve.wait_ge(turned_copied, NG * TURNS)
            then(V.reciprocal(rdegree, degree))
            dve.wait_ge(unscale_ready, 2)
            V.tensor_scalar(rdegree, rdegree, scale[:, 3:4], None, ALU.mult).then_inc(rdegree_ready, 1)
            dve.wait_ge(rdegree_ready, 1)

            def join(q, t, n, nodes, loads, b):
                row = y[0:nodes, n, :]
                dve.wait_ge(out_summed, q + 1)
                dve.wait_ge(res_in[n], loads)
                V.scalar_tensor_tensor(out=row, in0=b[0:nodes, 0:D], scalar=rdegree[0:nodes, bass.ds(t, 1)],
                                       in1=row, op0=ALU.mult, op1=ALU.add).then_inc(high_joined, 1)
                dve.wait_ge(high_joined, q + 1)
                V.scalar_tensor_tensor(out=row, in0=b[0:nodes, D:2 * D], scalar=rdegree[0:nodes, bass.ds(t, 1)],
                                       in1=row, op0=ALU.mult, op1=ALU.add).then_inc(bank_read, 1)
                dve.wait_ge(bank_read, q + 1)
                V.bn_stats(stats[0:nodes, n, :], row).then_inc(stats_ready, 1)

            def root(q, n, nodes):
                dve.wait_ge(root_ready, q + 1)
                V.reciprocal(deviation[0:nodes, n, 1:2], deviation[0:nodes, n, 0:1]).then_inc(root_inverted, 1)

            def aggregate_stats(n, nodes):
                V.bn_aggr(moments[0:nodes, n, :], stats[0:nodes, n, :]).then_inc(moments_ready, 1)

            def factor(q, n, nodes):
                dve.wait_ge(root_inverted, q + 1)
                V.scalar_tensor_tensor(out=deviation[0:nodes, n, 2:3], in0=moments[0:nodes, n, 0:1], scalar=-1.0,
                                       in1=deviation[0:nodes, n, 1:2], op0=ALU.mult, op1=ALU.mult)\
                    .then_inc(factors_ready, 1)

            def finish(q, t, n, nodes, loads, b, before=P):
                join(q, t, n, nodes, loads, b)
                dve.wait_ge(stats_ready, q + 1)
                root(q - 1, (n - 1) % TPS, before)
                aggregate_stats(n, nodes)
                factor(q - 1, (n - 1) % TPS, before)

            join(0, 2 * TPS, 0, P, 16, bank[0])
            dve.wait_ge(stats_ready, 1)
            aggregate_stats(0, P)
            for q in range(1, 2 * TPS):
                finish(q, 2 * TPS + q, q % TPS, P, 16 * (q // TPS + 1), bank[q])
            with dve.Fori(2, NFULL - 2) as g:
                for n in range(TPS):
                    finish(g * TPS + n, (g + 2) * TPS + n, n, P, g * 16 + 16, bank[n])
            for q in range(LOOPED, ST):
                s, n, nodes = tile_of(q)
                finish(q, s * TPS + n, q % TPS, nodes, 16 * (q // TPS + 1), bank[TPS + q % TPS], tile_of(q - 1)[2])
            root(ST - 1, (ST - 1) % TPS, P)
            factor(ST - 1, (ST - 1) % TPS, P)

        @block.scalar
        def _(act):
            A = nc.scalar
            act.wait_ge(eps_ready, 1)
            A.copy(warm, eps)

            def load_weights():
                act.dma_start(w1_in[:, 0], w1l.rearrange("(m p) f -> p m f", p=P)).then_inc(w_in, 16)
                act.dma_start(w1_in[:, 1], w1r.rearrange("(m p) f -> p m f", p=P)).then_inc(w_in, 16)
                act.dma_start(w2_in[:, 0], w2l.rearrange("(o p) h -> p o h", p=P)).then_inc(w_in, 16)
                act.dma_start(w2_in[:, 1], w2r.rearrange("(o p) h -> p o h", p=P)).then_inc(w_in, 16)
                act.dma_start(b1T, b1l.rearrange("(m p) -> p m", p=P),
                              allow_slow_non_contiguous=True).then_inc(bias_in, 16)

            def high_part(value, nodes, t0, n, which):
                return A.activation(parts[0:nodes, t0:t0 + n, 0:D], value, ACT.Copy,
                                    scale=scale[0:nodes, which:which + 1])

            def split_x(c):
                act.wait_ge(x_scaled, c + 1)
                A.copy(parts[:, c * XC:(c + 1) * XC, 0:D], x_in[:, c * XC:(c + 1) * XC, :]).then_inc(high_ready, 1)

            def unmix(g):
                act.wait_ge(gathered, (g * RPC + RPC) * 16)
                A.copy(unmixed[0:GS].rearrange("p k (i e) -> p k i e", e=ROW),
                       rows[0:GS].rearrange("p i k e -> p k i e")).then_inc(rows_unmixed, 1)

            def copy_weights(k):
                w1T, w2T = split_weights(weights_first)
                act.wait_ge(w_turned, k + 1)
                to = w1T[:, k, :] if k < 2 * FT else w2T[:, k - 2 * FT, :]
                A.copy(to, bank[WEIGHTS[k % 2]]).then_inc(w_copied, 1)

            def store_window(where, w, b, done, done_strip=None):
                act.wait_ge(window_summed, done + 1)
                A.copy(where[:, :, bass.ds(w * WIN, WIN)].rearrange("p t (u c) -> p t u c", c=PANE),
                       windows(bank[BUILT[b]]))
                if w == 0 and done_strip is not None:
                    act.wait_ge(degree_summed, done_strip)
                A.copy(column_sums[:, w * WIN:(w + 1) * WIN].rearrange("p (u c) -> p u c", c=PANE),
                       window_columns(bank[BUILT[b]])).then_inc(window_stored, 1)

            def store_pane(where, w, done):
                act.wait_ge(all_summed, done + 1)
                A.copy(where[:, :, bass.ds(w * PANE, PANE)],
                       bank[BUILT[0]][:, 0:KEYS].rearrange("p (t c) -> p t c", c=PANE)).then_inc(all_stored, 1)

            def follow(s, plan, kind, b):
                tiles, nodes, cols = tiles_of(kind)
                where = None if kind >= NFULL else last_strip if kind == NFULL - 1 else strip(b)
                for what, n in plan:
                    if what == "W":
                        store_window(where, n, n % 2, b * WPS + n, b)
                    elif what == "G":
                        act.wait_ge(turned, s * TURNS + TURNS)
                        A.copy(degree[0:nodes, bass.ds(s * TPS, tiles)], bank[TURN][0:nodes, 0:tiles])\
                            .then_inc(turned_copied, 1)
                        if any(x == "R" for x, _ in plan):
                            unmix_next(s)
                    elif what == "X":
                        act.wait_ge(turned, s * TURNS + n + 1)
                        if kind == 0 and n == 0:
                            act.wait_ge(early_out[0], 16)
                        A.copy(xT[:, n, 0:cols], bank[TURN][:, 0:cols]).then_inc(turned_copied, 1)
                    elif what == "H" and n[1]:
                        m = n[0]
                        if kind and m == 0:
                            act.wait_ge(zr_summed, s * TPS)
                        act.wait_ge(h_summed, s * HT + m + 1)
                        A.activation(hT[:, m, 0:cols], bank[HID[m % 2]][:, 0:cols], ACT.Relu, bias=b1T[:, m:m + 1])\
                            .then_inc(h_ready, 1)
                    elif what == "Z" and n[1]:
                        n = n[0]
                        act.wait_ge(zr_summed, s * TPS + n + 1)
                        if kind:
                            act.wait_ge(z_stored[n % 2], s * (16 * TPS // 2) + 16 * (n // 2))
                        elif n >= 2:
                            act.wait_ge(z_stored[n % 2], 16 * (n // 2))
                        A.copy(z_out[0:nodes, n % 2, :], bank[ZR[n % 2]][0:nodes, 0:D]).then_inc(z_copied, 1)

            def unmix_next(s):
                act.wait_ge(rows_turned, s + 2)
                unmix(s + 2)

            def steps_of(build):
                run_layers(act, lambda s, plan, kind: follow(s, plan, kind, s + 1), build)

            act.wait_ge(flag_ready, 1)
            slow = act.value_load(flag[0:1, 0:1])
            with act.If(slow > 0):
                load_weights()
                for c in range(NSPLIT):
                    split_x(c)
                for k in range(WBANKS):
                    copy_weights(k)
                act.wait_ge(low_ready, NSPLIT)
                act.wait_ge(w_stored, 16)
                with act.Fori(0, NFULL) as s:
                    with act.Fori(0, WPS * PPW) as w:
                        store_pane(strip(s), w, s * (WPS * PPW) + w)
                with act.Fori(0, WLAST * PPW) as w:
                    store_pane(last_strip, w, w + NFULL * WPS * PPW)
                act.wait_ge(bias_in, 16)
                steps_of(False)
            with act.Else():
                for what, n in first_plan():
                    if what == "W":
                        store_window(strip(0), n, n % 2, n)
                    elif what == "S":
                        split_x(n)
                    elif what == "T":
                        copy_weights(n)
                    elif what == "U":
                        if n:
                            act.wait_ge(rows_turned, n)
                        unmix(n)
                        if n == 0:
                            load_weights()
                act.wait_ge(bias_in, 16)
                steps_of(True)

            act.wait_ge(scale_ready, 2)
            for c in range(NSPLIT):
                if c == 0:
                    act.wait_ge(z_loaded[0], 16)
                    high_part(z_in[0][:, 0:1, :], P, 0, 1, 1).then_inc(high_ready, 1)
                    high_part(z_in[0][:, 1:XC, :], P, 1, XC - 1, 1).then_inc(high_ready, 1)
                elif c < NSPLIT - 1:
                    act.wait_ge(z_loaded[c % 2], 16 * (c // 2 + 1))
                    high_part(z_in[c % 2], P, c * XC, XC, 1).then_inc(high_ready, 1)
                else:
                    act.wait_ge(z_loaded[c % 2], 16 * (c // 2 + 2))
                    high_part(z_in[c % 2][:, 0:XC - 1, :], P, c * XC, XC - 1, 1)
                    high_part(z_in[c % 2][0:NLAST, XC - 1:XC, :], NLAST, ST - 1, 1, 1).then_inc(high_ready, 1)

            def norm(q, n, nodes):
                act.wait_ge(moments_ready, q + 1)
                A.activation(deviation[0:nodes, n, 0:1], moments[0:nodes, n, 1:2], ACT.Sqrt, bias=eps[0:nodes, :])\
                    .then_inc(root_ready, 1)
                act.wait_ge(factors_ready, q + 1)
                A.activation(y[0:nodes, n, :], y[0:nodes, n, :], ACT.Identity, scale=deviation[0:nodes, n, 1:2],
                             bias=deviation[0:nodes, n, 2:3]).then_inc(normed, 1)

            with act.Fori(0, NFULL - 2) as g:
                for n in range(TPS):
                    norm(g * TPS + n, n, P)
            for q in range(LOOPED, ST):
                norm(q, q % TPS, tile_of(q)[2])

        @block.tensor
        def _(pe):
            T = nc.tensor

            def mm(o, a, b, start=True, stop=True):
                return T.matmul(o, a, b, start=start, stop=stop)

            pe.wait_ge(consts, 4)
            for t in range(TR):
                pe.wait_ge(below_ready, t + 1)
                ins = mm(bank[DEG][0:1, 0:NPANE + 1], ones16[:, 0:1], starts_below[:, t, :], t == 0, t == TR - 1)
            ins.then_inc(rows_counted, 1)
            pe.wait_ge(slot_row_ready, 1)
            for g in range(NG):
                ins = mm(bank[DEG][0:GS, 320 + g * RPC:320 + (g + 1) * RPC], slot_row[0:1, g * GS:(g + 1) * GS],
                         ones16[0:1, 0:RPC])
            ins.then_inc(slot_row_turned, 1)
            pe.wait_ge(order_ready, 1)
            pe.wait_ge(index_ready, 1)
            mm(bank[DEG][0:1, 256:257], odd, ones[:, 0:1]).then_inc(order_summed, 1)

            def turn_maxima(which):
                pe.wait_ge(xmax_ready if which == 0 else zmax_ready, 1)
                T.transpose(bank[DEG][0:1, 0:P], amax[:, which:which + 1], ident).then_inc(max_turned, 1)

            def spread_scale(which):
                pe.wait_ge(scale_row, which + 1)
                mm(bank[DEG][:, 256:257], ones[0:1, :], srow[0:1, 3:4]).then_inc(scale_spread, 1)

            def turn_weights(k):
                if k == 0:
                    pe.wait_ge(w_in, 4 * 16)
                if k >= 2:
                    pe.wait_ge(w_copied, k - 1)
                for i in range(4):
                    if k < 2 * FT:
                        tile = w1_in[:, k // FT, i, (k % FT) * P:(k % FT + 1) * P]
                    else:
                        tile = w2_in[:, i // FT, i % FT, (k - 2 * FT) * P:(k - 2 * FT + 1) * P]
                    ins = T.transpose(bank[WEIGHTS[k % 2]][:, i * P:(i + 1) * P], tile, ident)
                ins.then_inc(w_turned, 1)

            def turn_rows(g):
                pe.wait_ge(rows_unmixed, g + 1)
                for k in range(2):
                    ins = T.transpose(bank[TURN][:, k * P:k * P + GS], unmixed[0:GS, k, :], ident[0:GS, 0:GS])
                ins.then_inc(rows_turned, 1)

            def sum_window(b, k):
                if not (isinstance(b, int) and b == 0 and k < 2):
                    pe.wait_ge(window_stored, b * WPS + (k - 1))
                for j in range(CPW):
                    pe.wait_ge(hot_ready, b * GS + (k * CPW + j + 1))
                    u = j // CH
                    ins = mm(bank[BUILT[k % 2]][:, u * COLS:(u + 1) * COLS], hot_src[:, k % 2, :, j],
                             hot_key[:, (k % 2) * CPW + j, :], j % CH == 0, j % CH == CH - 1)
                ins.then_inc(window_summed, 1)

            def sum_tile(where, t, a, cols):
                for k in range(FT):
                    for part in range(2):
                        c = part * D + k * P
                        ins = mm(bank[AGG[k]][:, a:a + cols], parts[:, t, c:c + P], where[:, t, a:a + cols],
                                 t == 0 and part == 0, t == ST - 1 and part == 1)
                return ins

            def sum_quarter(q, t, built):
                if t == 0 and built:
                    pe.wait_ge(window_stored, (q + 1) * WPQ)
                if q == 0 and t % XC == 0:
                    pe.wait_ge(low_ready, t // XC + 1)
                ins = sum_tile(strip(0), t, q * QUARTER, QUARTER)
                if q == TPS - 1 and t == ST - 1:
                    ins.then_inc(agg_summed, 1)

            def follow(s, plan, kind, b, build, weights_):
                tiles, nodes, cols = tiles_of(kind)
                where = last_strip if kind == NFULL else strip(s)
                w1T, w2T = split_weights(weights_)
                for what, n in plan:
                    if what == "W":
                        sum_window(b, n)
                    elif what == "R":
                        pe.wait_ge(turned_copied, s * TURNS + TURNS)
                        turn_rows(s + 2)
                    elif what == "Q":
                        sum_quarter(*n, build)
                    elif what == "D":
                        if build:
                            pe.wait_ge(window_stored, NWIN if kind == NFULL else s * WPS + WPS)
                        else:
                            pe.wait_ge(columns_summed, s + 1)
                        if kind:
                            pe.wait_ge(degree_ready, s)
                        mm(bank[DEG][:, 0:cols], ones, column_sums[:, 0:cols]).then_inc(degree_summed, 1)
                    elif what == "A":
                        if n == 0:
                            if kind:
                                pe.wait_ge(r_added, s * TPS)
                        ins = sum_tile(where, n, 0, cols)
                        if n == ST - 1:
                            ins.then_inc(agg_summed, 1)
                    elif what == "G":
                        pe.wait_ge(degree_ready, s + 1)
                        pe.wait_ge(turned_copied, s * TURNS + FT)
                        row = degrees_of(kind, build)[0]
                        for i in range(tiles):
                            ins = mm(bank[TURN][0:nodes, i:i + 1], row[0:1, i * P:i * P + nodes], ones[0:1, 0:1])
                        ins.then_inc(turned, 1)
                    elif what == "X":
                        if kind == NFULL:
                            pe.wait_ge(last_x_in, 16)
                        else:
                            pe.wait_ge(xs_in, s * 16 + 16)
                        if n == 0 and build:
                            pe.wait_ge(slots_ready, s + 2 if kind < NFULL else NG)
                        if n or kind:
                            pe.wait_ge(turned_copied, s * TURNS + n)
                        for i in range(tiles):
                            ins = T.transpose(bank[TURN][:, i * P:i * P + nodes],
                                              xs_of(kind)[0:nodes, i, n * P:(n + 1) * P], ident[0:nodes, 0:nodes])
                        ins.then_inc(turned, 1)
                    elif what == "H":
                        m, half = n
                        if half == 0 and m == 0:
                            pe.wait_ge(turned_copied, s * TURNS + FT)
                        elif half == 0 and m >= 2:
                            pe.wait_ge(h_ready, s * HT + (m - 1))
                        for k in range(FT):
                            if half and m == 0:
                                pe.wait_ge(agg_ready, s * FT + k + 1)
                            ins = mm(bank[HID[m % 2]][:, 0:cols], w1T[:, k if half else FT + k, m * P:(m + 1) * P],
                                     aggT[:, k, 0:cols] if half else xT[:, k, 0:cols],
                                     half == 0 and k == 0, half == 1 and k == FT - 1)
                        if half:
                            ins.then_inc(h_summed, 1)
                    elif what == "Z":
                        n, half = n
                        if half == 0 and n == 0:
                            pe.wait_ge(h_ready, s * HT + HT // 2)
                        if half == 1 and n == 0:
                            pe.wait_ge(h_ready, s * HT + HT)
                        if half == 0 and n >= 2:
                            pe.wait_ge(r_added, s * TPS + (n - 1))
                        for m in range(half * HT // 2, (half + 1) * HT // 2):
                            ins = mm(bank[ZR[n % 2]][0:nodes, :], hT[:, m, n * P:n * P + nodes], w2T[:, m, :],
                                     m == 0, m == HT - 1)
                        if half:
                            ins.then_inc(zr_summed, 1)

            def steps_of(build):
                def step(s, plan, kind):
                    if kind == 2:
                        pe.wait_ge(w_back, 16 if build else 32)
                    follow(s, plan, kind, s + 1, build,
                           weights_later if kind >= 2 else weights_first if build else work)
                run_layers(pe, step, build)

            pe.wait_ge(flag_ready, 1)
            slow = pe.value_load(flag[0:1, 0:1])
            with pe.If(slow > 0):
                turn_maxima(0)
                spread_scale(0)
                for k in range(WBANKS):
                    turn_weights(k)
                pe.wait_ge(consts, 12)
                one = bank[BUILT[0]][:, 0:KEYS]
                mm(one, zero16, iota_key).then_inc(all_used, 1)
                with pe.Fori(0, NPANE) as w:
                    mm(one, zero16, iota_key, True, False)
                    with pe.Fori(0, EC // CPW) as c:
                        pe.wait_ge(all_hot, w * (EC // CPW) + c + 1)
                        for j in range(CPW):
                            ins = mm(one, hot_src[:, 0, :, j], hot_key[:, j, 0:KEYS], False, False)
                        ins.then_inc(all_used, 1)
                    mm(one, zero16, iota_key, False, True).then_inc(all_summed, 1)
                    pe.wait_ge(all_stored, w + 1)
                for q in range(TPS - 1):
                    for t in range(ST):
                        sum_quarter(q, t, False)
                pe.wait_ge(w_back, 16)
                steps_of(False)
            with pe.Else():
                turn_rows(0)
                turn_maxima(0)
                for what, n in first_plan():
                    if what == "W":
                        sum_window(0, n)
                    elif what == "T":
                        turn_weights(n)
                    elif what == "P":
                        spread_scale(0)
                    elif what in "SU":
                        continue
                    elif what == "R":
                        pe.wait_ge(slots_ready, 1)
                        turn_rows(1)
                    else:
                        sum_quarter(*n, True)
                steps_of(True)

            turn_maxima(1)
            spread_scale(1)

            def sum_out(q, where, col, nodes, b, free=True):
                if free:
                    pe.wait_ge(bank_read, q - 3)
                for t in range(ST):
                    ins = mm(b[0:nodes, :], where[:, t, col:col + nodes], parts[:, t, :], t == 0, t == ST - 1)
                ins.then_inc(out_summed, 1)

            pe.wait_ge(scale_ready, 2)
            for t in range(ST):
                if t == 0:
                    pe.wait_ge(low_ready, NSPLIT + 1)
                elif t == 1 or t % XC == 0:
                    pe.wait_ge(low_ready, NSPLIT + t // XC + 2)
                for n in range(TPS):
                    ins = mm(bank[n], strip(2)[:, t, n * P:(n + 1) * P], parts[:, t, :], t == 0, t == ST - 1)
                    if t == ST - 1:
                        ins.then_inc(out_summed, 1)
            for n in range(TPS):
                sum_out(TPS + n, strip(3), n * P, P, bank[TPS + n], False)
            with pe.Fori(2, NFULL - 2) as g:
                for n in range(TPS):
                    sum_out(g * TPS + n, strip(g + 2), n * P, P, bank[n])
            for q in range(LOOPED, ST):
                s, n, nodes = tile_of(q)
                if q == LOOPED + 1:
                    pe.wait_ge(early_back, 16)
                sum_out(q, last_strip if s == NFULL else strip(s), n * P, nodes, bank[TPS + q % TPS])


_INS = ["x", "src", "dst", "L0_gnn_W1l", "L0_gnn_b1l", "L0_gnn_W1r", "L0_gnn_W2l", "L0_gnn_b2l", "L0_gnn_W2r"]


def kernel(**inputs):
    import numpy as _np
    import concourse.bacc as _bacc
    from concourse import mybir as _mybir
    from concourse.bass_utils import run_bass_kernel_spmd as _run

    nc = _bacc.Bacc("TRN2", target_bir_lowering=False, num_devices=1)
    arrays, args = {}, []
    for name in _INS:
        a = _np.ascontiguousarray(inputs[name])
        arrays[f"in_{name}"] = a
        args.append(nc.dram_tensor(f"in_{name}", a.shape, _mybir.dt.from_np(a.dtype), kind="ExternalInput").ap())
    shape = inputs["x"].shape
    args.append(nc.dram_tensor("out_dram", shape, _mybir.dt.float32, kind="ExternalOutput").ap())
    bass_sage_resnorm(nc, *args)
    r = _run(nc, [arrays], core_ids=[0])
    return r.results[0]["out_dram"]
```
